# Optimizing a Trainium2 kernel written in Bass

```python
import numpy as np
import jax
import jax.numpy as jnp

def _softmax(x, axis=-1):
    return jax.nn.softmax(x, axis=axis)

def _gelu(x):
    return jax.nn.gelu(x, approximate=True)

def _silu(x):
    return jax.nn.silu(x)

def _sigmoid(x):
    return jax.nn.sigmoid(x)

def _layernorm(x, axis=-1, eps=1e-05):
    m = jnp.mean(x, axis=axis, keepdims=True)
    v = jnp.var(x, axis=axis, keepdims=True)
    return (x - m) / jnp.sqrt(v + eps)

def _scatter_add(tgt, idx, src, axis=0):
    return tgt.at[idx].add(src)

def _segment_sum(src, seg, n):
    return jax.ops.segment_sum(src, seg, n)
kernel_name = 'mk_dlrm_tower_d1_rec_r8_0eab2f'

def setup_inputs(seed: int=0):
    np.random.seed(seed)
    _w = jnp.asarray

    def _rec_inputs():
        import jax
        import jax.numpy as jnp
        _tk = jax.random.key(seed)
        dense_ctx = jax.random.normal(jax.random.fold_in(_tk, 190), (512, 16), jnp.float32)
        ids = jnp.stack([jax.random.randint(jax.random.fold_in(_tk, 200 + f), (512,), 0, v, jnp.int32) for f, v in enumerate([1250, 1250, 125000, 12500, 12500, 125000, 12500, 12500, 12500, 1000, 1250, 1000, 1000, 1250, 1000, 12500, 125000, 12500, 12500, 1250, 12500, 125000, 1250, 1000, 12500, 125000, 1250, 1000, 1000, 1250, 1250, 125000, 12500, 1000, 1000, 1000, 1250, 1250, 12500, 1250])], axis=1)
        tbl_0 = 0.05 * jax.random.normal(jax.random.fold_in(_tk, 500 + 0), (1250, 32), jnp.float32)
        tbl_1 = 0.05 * jax.random.normal(jax.random.fold_in(_tk, 500 + 1), (1250, 32), jnp.float32)
        tbl_2 = 0.05 * jax.random.normal(jax.random.fold_in(_tk, 500 + 2), (125000, 32), jnp.float32)
        tbl_3 = 0.05 * jax.random.normal(jax.random.fold_in(_tk, 500 + 3), (12500, 32), jnp.float32)
        tbl_4 = 0.05 * jax.random.normal(jax.random.fold_in(_tk, 500 + 4), (12500, 32), jnp.float32)
        tbl_5 = 0.05 * jax.random.normal(jax.random.fold_in(_tk, 500 + 5), (125000, 32), jnp.float32)
        tbl_6 = 0.05 * jax.random.normal(jax.random.fold_in(_tk, 500 + 6), (12500, 32), jnp.float32)
        tbl_7 = 0.05 * jax.random.normal(jax.random.fold_in(_tk, 500 + 7), (12500, 32), jnp.float32)
        tbl_8 = 0.05 * jax.random.normal(jax.random.fold_in(_tk, 500 + 8), (12500, 32), jnp.float32)
        tbl_9 = 0.05 * jax.random.normal(jax.random.fold_in(_tk, 500 + 9), (1000, 32), jnp.float32)
        tbl_10 = 0.05 * jax.random.normal(jax.random.fold_in(_tk, 500 + 10), (1250, 32), jnp.float32)
        tbl_11 = 0.05 * jax.random.normal(jax.random.fold_in(_tk, 500 + 11), (1000, 32), jnp.float32)
        tbl_12 = 0.05 * jax.random.normal(jax.random.fold_in(_tk, 500 + 12), (1000, 32), jnp.float32)
        tbl_13 = 0.05 * jax.random.normal(jax.random.fold_in(_tk, 500 + 13), (1250, 32), jnp.float32)
        tbl_14 = 0.05 * jax.random.normal(jax.random.fold_in(_tk, 500 + 14), (1000, 32), jnp.float32)
        tbl_15 = 0.05 * jax.random.normal(jax.random.fold_in(_tk, 500 + 15), (12500, 32), jnp.float32)
        tbl_16 = 0.05 * jax.random.normal(jax.random.fold_in(_tk, 500 + 16), (125000, 32), jnp.float32)
        tbl_17 = 0.05 * jax.random.normal(jax.random.fold_in(_tk, 500 + 17), (12500, 32), jnp.float32)
        tbl_18 = 0.05 * jax.random.normal(jax.random.fold_in(_tk, 500 + 18), (12500, 32), jnp.float32)
        tbl_19 = 0.05 * jax.random.normal(jax.random.fold_in(_tk, 500 + 19), (1250, 32), jnp.float32)
        tbl_20 = 0.05 * jax.random.normal(jax.random.fold_in(_tk, 500 + 20), (12500, 32), jnp.float32)
        tbl_21 = 0.05 * jax.random.normal(jax.random.fold_in(_tk, 500 + 21), (125000, 32), jnp.float32)
        tbl_22 = 0.05 * jax.random.normal(jax.random.fold_in(_tk, 500 + 22), (1250, 32), jnp.float32)
        tbl_23 = 0.05 * jax.random.normal(jax.random.fold_in(_tk, 500 + 23), (1000, 32), jnp.float32)
        tbl_24 = 0.05 * jax.random.normal(jax.random.fold_in(_tk, 500 + 24), (12500, 32), jnp.float32)
        tbl_25 = 0.05 * jax.random.normal(jax.random.fold_in(_tk, 500 + 25), (125000, 32), jnp.float32)
        tbl_26 = 0.05 * jax.random.normal(jax.random.fold_in(_tk, 500 + 26), (1250, 32), jnp.float32)
        tbl_27 = 0.05 * jax.random.normal(jax.random.fold_in(_tk, 500 + 27), (1000, 32), jnp.float32)
        tbl_28 = 0.05 * jax.random.normal(jax.random.fold_in(_tk, 500 + 28), (1000, 32), jnp.float32)
        tbl_29 = 0.05 * jax.random.normal(jax.random.fold_in(_tk, 500 + 29), (1250, 32), jnp.float32)
        tbl_30 = 0.05 * jax.random.normal(jax.random.fold_in(_tk, 500 + 30), (1250, 32), jnp.float32)
        tbl_31 = 0.05 * jax.random.normal(jax.random.fold_in(_tk, 500 + 31), (125000, 32), jnp.float32)
        tbl_32 = 0.05 * jax.random.normal(jax.random.fold_in(_tk, 500 + 32), (12500, 32), jnp.float32)
        tbl_33 = 0.05 * jax.random.normal(jax.random.fold_in(_tk, 500 + 33), (1000, 32), jnp.float32)
        tbl_34 = 0.05 * jax.random.normal(jax.random.fold_in(_tk, 500 + 34), (1000, 32), jnp.float32)
        tbl_35 = 0.05 * jax.random.normal(jax.random.fold_in(_tk, 500 + 35), (1000, 32), jnp.float32)
        tbl_36 = 0.05 * jax.random.normal(jax.random.fold_in(_tk, 500 + 36), (1250, 32), jnp.float32)
        tbl_37 = 0.05 * jax.random.normal(jax.random.fold_in(_tk, 500 + 37), (1250, 32), jnp.float32)
        tbl_38 = 0.05 * jax.random.normal(jax.random.fold_in(_tk, 500 + 38), (12500, 32), jnp.float32)
        tbl_39 = 0.05 * jax.random.normal(jax.random.fold_in(_tk, 500 + 39), (1250, 32), jnp.float32)
        _rk = jax.random.fold_in(_tk, 7)
        W_top1 = 0.0354441 * jax.random.normal(jax.random.fold_in(_tk, 801), (796, 512), jnp.float32)
        W_top2 = 0.0441942 * jax.random.normal(jax.random.fold_in(_tk, 802), (512, 256), jnp.float32)
        W_top3 = 0.0625 * jax.random.normal(jax.random.fold_in(_tk, 803), (256, 1), jnp.float32)
        b_top1 = jnp.zeros((512,), jnp.float32)
        b_top2 = jnp.zeros((256,), jnp.float32)
        return (dense_ctx, ids, tbl_0, tbl_1, tbl_2, tbl_3, tbl_4, tbl_5, tbl_6, tbl_7, tbl_8, tbl_9, tbl_10, tbl_11, tbl_12, tbl_13, tbl_14, tbl_15, tbl_16, tbl_17, tbl_18, tbl_19, tbl_20, tbl_21, tbl_22, tbl_23, tbl_24, tbl_25, tbl_26, tbl_27, tbl_28, tbl_29, tbl_30, tbl_31, tbl_32, tbl_33, tbl_34, tbl_35, tbl_36, tbl_37, tbl_38, tbl_39, W_top1, b_top1, W_top2, b_top2, W_top3)
    dense_ctx, ids, tbl_0, tbl_1, tbl_2, tbl_3, tbl_4, tbl_5, tbl_6, tbl_7, tbl_8, tbl_9, tbl_10, tbl_11, tbl_12, tbl_13, tbl_14, tbl_15, tbl_16, tbl_17, tbl_18, tbl_19, tbl_20, tbl_21, tbl_22, tbl_23, tbl_24, tbl_25, tbl_26, tbl_27, tbl_28, tbl_29, tbl_30, tbl_31, tbl_32, tbl_33, tbl_34, tbl_35, tbl_36, tbl_37, tbl_38, tbl_39, W_top1, b_top1, W_top2, b_top2, W_top3 = _rec_inputs()

    def _L0_rec_setup():
        import jax, jax.numpy as jnp
        import numpy as np
        NUM_FIELDS = 40
        _I_IDX, _J_IDX = np.triu_indices(NUM_FIELDS, k=1)
        key = jax.random.key(seed)
        k1, k2 = jax.random.split(key)
        batch, num_fields, embed_dim = (1024, NUM_FIELDS, 32)
        num_interactions = num_fields * (num_fields - 1) // 2
        embeddings = jax.random.normal(k1, (batch, num_fields, embed_dim), dtype=jnp.float32)
        W = jax.random.normal(k2, (num_interactions, embed_dim, embed_dim), dtype=jnp.float32)
        return {'embeddings': embeddings, 'W': W}
    _L0_rec_all = _L0_rec_setup()
    _L0_rec_in = {k: v for k, v in _L0_rec_all.items() if k in ('W',)}
    del _L0_rec_all
    return {'dense_ctx': dense_ctx, 'ids': ids, 'tbl_0': tbl_0, 'tbl_1': tbl_1, 'tbl_2': tbl_2, 'tbl_3': tbl_3, 'tbl_4': tbl_4, 'tbl_5': tbl_5, 'tbl_6': tbl_6, 'tbl_7': tbl_7, 'tbl_8': tbl_8, 'tbl_9': tbl_9, 'tbl_10': tbl_10, 'tbl_11': tbl_11, 'tbl_12': tbl_12, 'tbl_13': tbl_13, 'tbl_14': tbl_14, 'tbl_15': tbl_15, 'tbl_16': tbl_16, 'tbl_17': tbl_17, 'tbl_18': tbl_18, 'tbl_19': tbl_19, 'tbl_20': tbl_20, 'tbl_21': tbl_21, 'tbl_22': tbl_22, 'tbl_23': tbl_23, 'tbl_24': tbl_24, 'tbl_25': tbl_25, 'tbl_26': tbl_26, 'tbl_27': tbl_27, 'tbl_28': tbl_28, 'tbl_29': tbl_29, 'tbl_30': tbl_30, 'tbl_31': tbl_31, 'tbl_32': tbl_32, 'tbl_33': tbl_33, 'tbl_34': tbl_34, 'tbl_35': tbl_35, 'tbl_36': tbl_36, 'tbl_37': tbl_37, 'tbl_38': tbl_38, 'tbl_39': tbl_39, 'W_top1': W_top1, 'b_top1': b_top1, 'W_top2': W_top2, 'b_top2': b_top2, 'W_top3': W_top3, 'L0_rec_W': _L0_rec_in['W']}

def reference(dense_ctx, ids, tbl_0, tbl_1, tbl_2, tbl_3, tbl_4, tbl_5, tbl_6, tbl_7, tbl_8, tbl_9, tbl_10, tbl_11, tbl_12, tbl_13, tbl_14, tbl_15, tbl_16, tbl_17, tbl_18, tbl_19, tbl_20, tbl_21, tbl_22, tbl_23, tbl_24, tbl_25, tbl_26, tbl_27, tbl_28, tbl_29, tbl_30, tbl_31, tbl_32, tbl_33, tbl_34, tbl_35, tbl_36, tbl_37, tbl_38, tbl_39, W_top1, b_top1, W_top2, b_top2, W_top3, L0_rec_W):
    import jax
    import jax.numpy as jnp

    def _L0_rec_ref(embeddings, W):
        import jax, jax.numpy as jnp
        import numpy as np
        NUM_FIELDS = 40
        _I_IDX, _J_IDX = np.triu_indices(NUM_FIELDS, k=1)
        vi = embeddings[:, _I_IDX, :]
        vj = embeddings[:, _J_IDX, :]
        return jnp.einsum('bke,kef,bkf->bk', vi, W, vj)
    e = jnp.stack([tbl_0[ids[:, 0]], tbl_1[ids[:, 1]], tbl_2[ids[:, 2]], tbl_3[ids[:, 3]], tbl_4[ids[:, 4]], tbl_5[ids[:, 5]], tbl_6[ids[:, 6]], tbl_7[ids[:, 7]], tbl_8[ids[:, 8]], tbl_9[ids[:, 9]], tbl_10[ids[:, 10]], tbl_11[ids[:, 11]], tbl_12[ids[:, 12]], tbl_13[ids[:, 13]], tbl_14[ids[:, 14]], tbl_15[ids[:, 15]], tbl_16[ids[:, 16]], tbl_17[ids[:, 17]], tbl_18[ids[:, 18]], tbl_19[ids[:, 19]], tbl_20[ids[:, 20]], tbl_21[ids[:, 21]], tbl_22[ids[:, 22]], tbl_23[ids[:, 23]], tbl_24[ids[:, 24]], tbl_25[ids[:, 25]], tbl_26[ids[:, 26]], tbl_27[ids[:, 27]], tbl_28[ids[:, 28]], tbl_29[ids[:, 29]], tbl_30[ids[:, 30]], tbl_31[ids[:, 31]], tbl_32[ids[:, 32]], tbl_33[ids[:, 33]], tbl_34[ids[:, 34]], tbl_35[ids[:, 35]], tbl_36[ids[:, 36]], tbl_37[ids[:, 37]], tbl_38[ids[:, 38]], tbl_39[ids[:, 39]]], axis=1)
    z = _L0_rec_ref(e, L0_rec_W)
    z = z.reshape(z.shape[0], -1)
    h = jnp.concatenate([z, dense_ctx], axis=1)
    h = jnp.maximum(h @ W_top1 + b_top1, 0.0)
    h = jnp.maximum(h @ W_top2 + b_top2, 0.0)
    y = h @ W_top3
    return y

_drawn_inputs = setup_inputs


def setup_inputs(seed=0):
    import zlib

    import numpy as np

    out = dict(_drawn_inputs(seed))
    spreads = {'b_top1': (0.0, 0.1), 'b_top2': (0.0, 0.1)}
    factors = {}
    for name, (base, spread) in spreads.items():
        noise = np.random.default_rng([zlib.crc32(name.encode()), seed]).standard_normal(out[name].shape)
        drawn = base * np.exp(spread * noise) if base else spread * noise
        out[name] = jnp.asarray(drawn.astype(out[name].dtype))
    for name, factor in factors.items():
        out[name] = (out[name] * factor).astype(out[name].dtype)
    return out
```

```python
from contextlib import ExitStack

import concourse.bass as bass
import numpy as np
from concourse import mybir

F32 = mybir.dt.float32
F32R = mybir.dt.float32r
I32 = mybir.dt.int32
ALU = mybir.AluOpType
ACT = mybir.ActivationFunctionType

P = 128
BATCH = 512
CHUNKS = BATCH // P
FIELDS = 40
DIM = 32
SLOTS = P // DIM
QUADS = FIELDS // SLOTS
CTX = 16
HID1, HID2 = 512, 256
M1, M2 = HID1 // P, HID2 // P

ORDER = list(range(FIELDS))

RING_U = 2
RING_P = 4
RING_SPLIT = 4
RING_STREAM = 8
RING_W = 5
WCHUNKS = 11


def plan():
    ops_of = []
    for n in range(FIELDS):
        q, r = divmod(n, SLOTS)
        full = [(Q, [(n, tuple(range(SLOTS)))]) for Q in range(q)]
        ops = [full[i:i + 2] for i in range(0, len(full), 2)]
        if r == SLOTS - 1:
            a = SLOTS * q
            ops.append([(q, [(a + 3, (0, 1, 2))]), (q, [(a + 1, (0,)), (a + 2, (1,)), (a, (2,))])])
        ops_of.append(ops)
    return ops_of


OPS_OF = plan()
OPS = [op for ops in OPS_OF for op in ops]
TILES = [tile for op in OPS for tile in op]
FIRST_TILE = [sum(len(op) for op in OPS[:o]) for o in range(len(OPS))]
BLOCKS = [(t, stream, slots) for t, (quad, blocks) in enumerate(TILES) for stream, slots in blocks]
WBLOCKS = len(BLOCKS) // WCHUNKS
WPART = WBLOCKS // SLOTS
assert WBLOCKS * WCHUNKS == len(BLOCKS) and WPART * SLOTS == WBLOCKS

GROUP = DIM // SLOTS
ZTILE = SLOTS * GROUP
ZTILES = -(-len(TILES) // ZTILE)
CTX_ROW = 2 * SLOTS
assert (len(TILES) - ZTILE * (ZTILES - 1)) == CTX_ROW and CTX_ROW + CTX <= DIM


def z_place(t):
    return t // ZTILE, t % SLOTS, t % ZTILE // SLOTS


def pair_index(i, j):
    return i * FIELDS - i * (i + 1) // 2 + j - i - 1


def build(nc, ctx_rows, ids, tables, w_pairs, eye, selectors, w1, b1, w2, b2, w3, out):
    with ExitStack() as ctx:
        def sb(name, shape, dt=F32):
            return ctx.enter_context(nc.sbuf_tensor(name, shape, dt))

        def ps(name, shape):
            return ctx.enter_context(nc.psum_tensor(name, shape, F32))

        def sem(name):
            return ctx.enter_context(nc.semaphore(name))

        idx = sb("idx", [P, CHUNKS, FIELDS], I32)
        rows = sb("rows", [P, CHUNKS, FIELDS, DIM])
        split = sb("split", [P, RING_SPLIT, CHUNKS, 4, DIM], F32R)
        emb = sb("emb", [P, QUADS, BATCH])
        stream = sb("stream", [P, RING_STREAM, BATCH], F32R)
        wdense = sb("wdense", [P, 2, WPART * P])
        whi = sb("whi", [P, 2, WPART * P], F32R)
        wlo = sb("wlo", [P, 2, WPART * P], F32R)
        wstack = sb("wstack", [P, RING_W, WBLOCKS * P], F32R)
        prod = sb("prod", [P, RING_P, 2 * BATCH])
        zt = sb("zt", [P, ZTILES, BATCH])
        w1_sb = sb("w1_sb", [P, ZTILES, HID1])
        w2_sb = sb("w2_sb", [P, M1, HID2])
        w3_sb = sb("w3_sb", [P, M2])
        b1_sb = sb("b1_sb", [P, M1])
        b2_sb = sb("b2_sb", [P, M2])
        ctx_sb = sb("ctx_sb", [DIM, BATCH])
        eye_sb = sb("eye_sb", [P, P])
        eye_r = sb("eye_r", [P, P], F32R)
        sel = sb("sel", [P, GROUP, DIM])
        h1 = sb("h1", [P, M1, BATCH])
        h1_act = sb("h1_act", [P, M1, BATCH])
        h2 = sb("h2", [P, M2, BATCH])
        y_sb = sb("y_sb", [1, BATCH])

        u_ps = [ps(f"u_ps{i}", [P, 2 * BATCH]) for i in range(RING_U)]
        z_ps = [ps(f"z_ps{i}", [P, BATCH]) for i in range(2)]
        turn_ps = ps("turn_ps", [P, BATCH])
        lin_ps = ps("lin_ps", [P, BATCH])

        ids_loaded = sem("ids_loaded")
        const_loaded = sem("const_loaded")
        mlp_loaded = sem("mlp_loaded")
        wload = [sem(f"wload{i}") for i in range(WCHUNKS)]
        wstacked = [sem(f"wstacked{i}") for i in range(WCHUNKS)]
        gathered = [sem(f"gathered{n}") for n in range(FIELDS)]
        eye_ready = sem("eye_ready")
        whi_done = sem("whi_done")
        wlo_done = sem("wlo_done")
        hi_done = sem("hi_done")
        lo_done = sem("lo_done")
        turned = sem("turned")
        landed = sem("landed")
        mapped = sem("mapped")
        weighted = sem("weighted")
        summed = sem("summed")
        ctx_placed = sem("ctx_placed")
        z_saved = sem("z_saved")
        lin_done = sem("lin_done")
        lin_saved = sem("lin_saved")
        last_added = sem("last_added")
        h1_ready = sem("h1_ready")
        h2_done = sem("h2_done")
        h2_ready = sem("h2_ready")
        y_done = sem("y_done")
        y_saved = sem("y_saved")
        stored = sem("stored")

        turn_of, turns = {}, 0
        for n in range(FIELDS):
            turn_of["field", n] = turns
            turns += 1
            if n % SLOTS == SLOTS - 1:
                turn_of["quad", n // SLOTS] = turns
                turns += 1
        op_index, o = [], 0
        for ops in OPS_OF:
            op_index.append(list(range(o, o + len(ops))))
            o += len(ops)
        NOPS = o
        LAST = NOPS - 1

        def op_of_tile(t):
            return max(o for o in range(NOPS) if FIRST_TILE[o] <= t)

        def last_op_of_chunk(c):
            return op_of_tile(BLOCKS[WBLOCKS * (c + 1) - 1][0])

        PARTS = [(0, 1, 2), (3, 4)]
        TAIL = (5, 6)
        turn_before = [max(op_index[n - 1][0], op_index[n - 1][-1] - 1) if n and op_index[n - 1] else
                       op_index[n][0] if op_index[n] else 0 for n in range(FIELDS)]
        for n in range(1, FIELDS):
            turn_before[n] = max(turn_before[n], turn_before[n - 1])

        turn_steps = [(turn_before[n] - 0.5, n, "turn", n) for n in range(FIELDS)]
        land_steps = [(turn_before[n] - 0.5, n, "land", n) for n in range(FIELDS)]
        split_steps = [(max(turn_before[n] - 3.5, turn_before[max(n - 1, 0)] - 0.5), n - 0.5, "split", n)
                       for n in range(FIELDS)]
        op_steps = [(o, 0, "op", o) for o in range(NOPS)]
        weight_steps = [(-0.5, c - 0.75, "weights", c) for c in range(RING_W + 2)]
        weight_steps += [(last_op_of_chunk(c - 2 - RING_W) + 14.4, 0, "weights", c)
                         for c in range(RING_W + 2, WCHUNKS)]
        lin_steps, lin_save_steps = [], []
        for part, ks in enumerate(PARTS):
            for m in range(M1):
                at = op_of_tile(ZTILE * (ks[-1] + 1) - 1) + 5 + 3 * m
                lin_steps.append((at + 0.2, 0, "layer1", (part, m)))
                lin_save_steps.append((at + 1.2, 0, "save1", (part, m)))
        sums_after = {o: [s for s in (o - 3, o - 2) if s >= 0] for o in range(1, NOPS, 2)}
        left_sums = [o for o in range(NOPS) if not any(o in x for x in sums_after.values())]
        z_steps = [(o + 0.3, 0, "save_z", t // ZTILE) for o, sums in sums_after.items() for s in sums
                   for t in range(FIRST_TILE[s], FIRST_TILE[s] + len(OPS[s])) if (t + 1) % ZTILE == 0]

        def last_op_of_quad(q):
            return op_index[SLOTS * q + SLOTS - 1][-1]

        free = u_ps[(LAST - 1) % 2]
        tail_ps = [lin_ps[:], turn_ps[:], free[:, :BATCH], free[:, BATCH:]]

        block = ctx.enter_context(nc.Block())

        @block.sync
        def _(sp):
            sp.dma_start(idx[:], ids.rearrange("(c p) f -> p c f", p=P)).then_inc(ids_loaded, 16)

            def load_weights(c):
                if c >= 2:
                    sp.wait_ge(wlo_done, c - 1)
                sp.dma_start(wdense[:, c % 2, :], w_pairs[c]).then_inc(wload[c], 16)

            def stack_weights(c):
                sp.wait_ge(whi_done, c + 1)
                sp.wait_ge(wlo_done, c + 1)
                if c >= RING_W:
                    sp.wait_ge(mapped, last_op_of_chunk(c - RING_W) + 1)
                n = WPART * P
                for k, part in enumerate((whi, wlo, whi, wlo)):
                    for q in range(SLOTS):
                        sp.dma_start(wstack[DIM * k:DIM * (k + 1), c % RING_W, q * n:(q + 1) * n].bitcast(F32),
                                     part[DIM * q:DIM * (q + 1), c % 2, :].bitcast(F32)).then_inc(wstacked[c], 16)

            load_weights(0)
            sp.dma_start(eye_sb[:], eye).then_inc(const_loaded, 16)
            sp.dma_start(sel[:], selectors).then_inc(const_loaded, 16)
            sp.dma_start(ctx_sb[:], ctx_rows).then_inc(const_loaded, 16)
            load_weights(1)
            for c in range(WCHUNKS):
                if c == RING_W:
                    sp.dma_start(w1_sb[:], w1.rearrange("k p n -> p k n")).then_inc(mlp_loaded, 16)
                    sp.dma_start(w2_sb[:], w2.rearrange("(k p) n -> p k n", p=P)).then_inc(mlp_loaded, 16)
                    sp.dma_start(w3_sb[:], w3).then_inc(mlp_loaded, 16)
                    sp.dma_start(b1_sb[:], b1).then_inc(mlp_loaded, 16)
                    sp.dma_start(b2_sb[:], b2).then_inc(mlp_loaded, 16)
                stack_weights(c)
                if c + 2 < WCHUNKS:
                    load_weights(c + 2)
            sp.wait_ge(y_saved, 1)
            sp.dma_start(out.rearrange("b o -> o b"), y_sb[:]).then_inc(stored, 16)
            sp.wait_ge(stored, 16)

        @block.gpsimd
        def _(pool):
            pool.wait_ge(ids_loaded, 16)
            for n, f in enumerate(ORDER):
                for c in range(CHUNKS):
                    nc.gpsimd.indirect_dma_start(
                        rows[:, c, n, :], None, tables[f],
                        bass.IndirectOffsetOnAxis(ap=idx[:, c, f:f + 1], axis=0)).then_inc(gathered[n], 16)

        @block.scalar
        def _(act):
            def weights(c):
                act.wait_ge(wload[c], 16)
                if c >= 2:
                    act.wait_ge(wstacked[c - 2], 16 * SLOTS * SLOTS)
                nc.scalar.activation(whi[:, c % 2, :], wdense[:, c % 2, :], ACT.Copy).then_inc(whi_done, 1)

            def split_field(n):
                if n >= RING_SPLIT:
                    act.wait_ge(turned, turn_of["field", n - RING_SPLIT] + 1)
                act.wait_ge(gathered[n], 16 * CHUNKS)
                twice = rows[:, :, n, :].unsqueeze(2).to_broadcast([P, CHUNKS, 2, DIM])
                nc.scalar.activation(split[:, n % RING_SPLIT, :, 0:2, :], twice, ACT.Copy).then_inc(hi_done, 1)

            def land(n):
                q, r = divmod(n, SLOTS)
                if q >= 2 and r == 0:
                    act.wait_ge(mapped, last_op_of_quad(q - 2) + 1)
                act.wait_ge(turned, turn_of["field", n] + 1)
                nc.scalar.activation(stream[:, n % RING_STREAM, :], turn_ps[:], ACT.Copy).then_inc(landed, 1)
                if r == SLOTS - 1:
                    act.wait_ge(turned, turn_of["quad", q] + 1)
                    nc.scalar.activation(emb[:, q, :], turn_ps[:], ACT.Copy).then_inc(landed, 1)

            def save_z(k):
                if k < ZTILES - 1:
                    act.wait_ge(summed, op_of_tile(ZTILE * (k + 1) - 1) + 1)
                else:
                    act.wait_ge(ctx_placed, 1)
                nc.scalar.activation(zt[:, k, :], z_ps[k % 2][:], ACT.Copy).then_inc(z_saved, 1)

            def layer1(part, m):
                if part == 0:
                    if m == 0:
                        act.wait_ge(mlp_loaded, 80)
                    act.wait_ge(lin_done, m + 1)
                    nc.scalar.activation(h1[:, m, :], lin_ps[:], ACT.Identity,
                                         bias=b1_sb[:, m:m + 1]).then_inc(lin_saved, 1)

            for _, _, kind, what in sorted(weight_steps + split_steps + land_steps + z_steps + lin_save_steps):
                if kind == "weights":
                    weights(what)
                elif kind == "split":
                    split_field(what)
                elif kind == "land":
                    land(what)
                elif kind == "save_z":
                    save_z(what)
                elif kind == "save1":
                    layer1(*what)
            save_z(ZTILES - 1)
            for m in range(M1):
                act.wait_ge(last_added, m + 1)
                nc.scalar.activation(h1_act[:, m, :], h1[:, m, :], ACT.Relu).then_inc(h1_ready, 1)
            for m in range(M2):
                act.wait_ge(h2_done, m + 1)
                nc.scalar.activation(h2[:, m, :], u_ps[LAST % 2][:, m * BATCH:(m + 1) * BATCH], ACT.Relu,
                                     bias=b2_sb[:, m:m + 1]).then_inc(h2_ready, 1)

        @block.vector
        def _(dve):
            dve.wait_ge(const_loaded, 48)
            nc.vector.tensor_copy(eye_r[:], eye_sb[:]).then_inc(eye_ready, 1)

            def weights(c):
                dve.wait_ge(whi_done, c + 1)
                nc.vector.tensor_tensor(wlo[:, c % 2, :], wdense[:, c % 2, :], whi[:, c % 2, :],
                                        ALU.subtract).then_inc(wlo_done, 1)

            def split_field(n):
                dve.wait_ge(hi_done, n + 1)
                twice = rows[:, :, n, :].unsqueeze(2).to_broadcast([P, CHUNKS, 2, DIM])
                nc.vector.tensor_tensor(split[:, n % RING_SPLIT, :, 2:4, :], twice,
                                        split[:, n % RING_SPLIT, :, 0:2, :], ALU.subtract).then_inc(lo_done, 1)

            def weight_op(o):
                op = OPS[o]
                quads = [quad for quad, _ in op]
                dve.wait_ge(landed, turn_of["quad", max(quads)] + 1)
                dve.wait_ge(mapped, o + 1)
                if o >= RING_P:
                    dve.wait_ge(summed, o - RING_P + 1)
                n = len(op) * BATCH
                if quads[-1] > quads[0] or len(op) == 1:
                    slots = emb[:, quads[0]:quads[-1] + 1, :]
                else:
                    slots = emb[:, quads[0]:quads[0] + 1, :].to_broadcast([P, 2, BATCH])
                shaped = "p (t b) -> p t b"
                nc.vector.tensor_tensor(prod[:, o % RING_P, :n].rearrange(shaped, b=BATCH),
                                        u_ps[o % RING_U][:, :n].rearrange(shaped, b=BATCH), slots,
                                        ALU.mult).then_inc(weighted, 1)

            def layer1(part, m):
                if part == 1:
                    dve.wait_ge(lin_done, M1 + m + 1)
                    nc.vector.tensor_tensor(h1[:, m, :], lin_ps[:], h1[:, m, :], ALU.add).then_inc(lin_saved, 1)

            for _, _, kind, what in sorted(weight_steps + split_steps + op_steps + lin_save_steps):
                if kind == "weights":
                    weights(what)
                elif kind == "split":
                    split_field(what)
                elif kind == "op":
                    weight_op(what)
                elif kind == "save1":
                    layer1(*what)
            for m in range(M1):
                dve.wait_ge(lin_done, len(PARTS) * M1 + m + 1)
                if m == 0:
                    dve.wait_ge(lin_saved, len(PARTS) * M1)
                nc.vector.tensor_tensor(h1[:, m, :], tail_ps[m], h1[:, m, :], ALU.add).then_inc(last_added, 1)
            dve.wait_ge(y_done, 1)
            nc.vector.tensor_copy(y_sb[:], lin_ps[0:1, :]).then_inc(y_saved, 1)

        @block.tensor
        def _(pe):
            used = [0]

            def turn(n):
                q, r = divmod(n, SLOTS)
                if n == 0:
                    pe.wait_ge(eye_ready, 1)
                pe.wait_ge(lo_done, n + 1)
                if n:
                    pe.wait_ge(landed, turn_of["field", n])
                for c in range(CHUNKS):
                    parts = split[:, n % RING_SPLIT, c].rearrange("p k d -> p (k d)")
                    mm = nc.tensor.matmul(turn_ps[:, c * P:(c + 1) * P], parts, eye_r[:], start=True, stop=True)
                mm.then_inc(turned, 1)
                if r == SLOTS - 1:
                    pe.wait_ge(landed, turn_of["quad", q])
                    for c in range(CHUNKS):
                        quad = rows[:, c, SLOTS * q:SLOTS * (q + 1), :].rearrange("p r d -> p (r d)")
                        mm = nc.tensor.matmul(turn_ps[:, c * P:(c + 1) * P], quad, eye_sb[:], start=True, stop=True)
                    mm.then_inc(turned, 1)

            def map_op(o):
                if o >= RING_U:
                    pe.wait_ge(weighted, o - RING_U + 1)
                for i, (quad, blocks) in enumerate(OPS[o]):
                    for b, (n, slots) in enumerate(blocks):
                        c, w = divmod(used[0], WBLOCKS)
                        if w == 0:
                            pe.wait_ge(wstacked[c], 16 * SLOTS * SLOTS)
                        pe.wait_ge(landed, turn_of["field", n] + 1)
                        mm = nc.tensor.matmul(u_ps[o % RING_U][:, i * BATCH:(i + 1) * BATCH],
                                              wstack[:, c % RING_W, w * P:(w + 1) * P],
                                              stream[:, n % RING_STREAM, :],
                                              start=b == 0, stop=b == len(blocks) - 1)
                        used[0] += 1
                return mm

            def sum_op(o):
                pe.wait_ge(weighted, o + 1)
                for i in range(len(OPS[o])):
                    t = FIRST_TILE[o] + i
                    k, g, m = z_place(t)
                    if t % ZTILE == 0 and k >= 2:
                        pe.wait_ge(z_saved, k - 1)
                    last = m == GROUP - 1 or (t >= len(TILES) - SLOTS and g > 0)
                    mm = nc.tensor.matmul(z_ps[k % 2][DIM * g:DIM * (g + 1), :], sel[:, m, :],
                                          prod[:, o % RING_P, i * BATCH:(i + 1) * BATCH], start=m == 0, stop=last)
                    if i == len(OPS[o]) - 1:
                        mm.then_inc(summed, 1)

            def layer1(bank, ks, m, start=True, stop=True):
                for k in ks:
                    mm = nc.tensor.matmul(bank, w1_sb[:, k, m * P:(m + 1) * P], zt[:, k, :],
                                          start=start and k == ks[0], stop=stop and k == ks[-1])
                return mm

            pe.wait_ge(const_loaded, 48)
            for _, _, kind, what in sorted(turn_steps + op_steps + lin_steps):
                if kind == "turn":
                    turn(what)
                elif kind == "op":
                    map_op(what).then_inc(mapped, 1)
                    for o in sums_after.get(what, ()):
                        sum_op(o)
                elif kind == "layer1":
                    part, m = what
                    if m == 0:
                        pe.wait_ge(z_saved, PARTS[part][-1] + 1)
                        pe.wait_ge(mlp_loaded, 80)
                    if part or m:
                        pe.wait_ge(lin_saved, part * M1 + m)
                    layer1(lin_ps[:], PARTS[part], m).then_inc(lin_done, 1)

            pe.wait_ge(z_saved, TAIL[0] + 1)
            pe.wait_ge(lin_saved, len(PARTS) * M1)
            pe.wait_ge(landed, turns)
            layer1(tail_ps[0], TAIL[:1], 0, stop=False)
            layer1(tail_ps[1], TAIL[:1], 1, stop=False)
            for o in left_sums[:-1]:
                sum_op(o)
            layer1(tail_ps[2], TAIL[:1], 2, stop=False)
            layer1(tail_ps[3], TAIL[:1], 3, stop=False)
            sum_op(LAST)
            nc.tensor.matmul(z_ps[(ZTILES - 1) % 2][0:DIM, :], eye_sb[0:DIM, 0:DIM], ctx_sb[:],
                             start=False, stop=True).then_inc(ctx_placed, 1)
            pe.wait_ge(z_saved, ZTILES)
            for m in range(M1):
                layer1(tail_ps[m], TAIL[1:], m, start=False).then_inc(lin_done, 1)
            for k in range(M1):
                pe.wait_ge(h1_ready, k + 1)
                for m in range(M2):
                    mm = nc.tensor.matmul(u_ps[LAST % 2][:, m * BATCH:(m + 1) * BATCH],
                                          w2_sb[:, k, m * P:(m + 1) * P], h1_act[:, k, :],
                                          start=k == 0, stop=k == M1 - 1)
                    if k == M1 - 1:
                        mm.then_inc(h2_done, 1)
            for k in range(M2):
                pe.wait_ge(h2_ready, k + 1)
                mm = nc.tensor.matmul(lin_ps[0:1, :], w3_sb[:, k:k + 1], h2[:, k, :], start=k == 0, stop=k == M2 - 1)
            mm.then_inc(y_done, 1)


def packed_weights(w):
    packed = np.zeros((len(BLOCKS), DIM, SLOTS, DIM), w.dtype)
    for b, (t, stream, slots) in enumerate(BLOCKS):
        quad = TILES[t][0]
        for s in slots:
            slot_field, stream_field = ORDER[SLOTS * quad + s], ORDER[stream]
            if slot_field < stream_field:
                packed[b, :, s] = w[pair_index(slot_field, stream_field)].T
            else:
                packed[b, :, s] = w[pair_index(stream_field, slot_field)]
    packed = packed.reshape(WCHUNKS, SLOTS, WPART, DIM, P).transpose(0, 1, 3, 2, 4)
    return np.ascontiguousarray(packed.reshape(WCHUNKS, P, WPART * P))


def packed_layer1(w):
    packed = np.zeros((ZTILES, P, w.shape[1]), w.dtype)
    for t, stream, slots in BLOCKS:
        k, g, m = z_place(t)
        for s in slots:
            i, j = sorted((ORDER[SLOTS * TILES[t][0] + s], ORDER[stream]))
            packed[k, DIM * g + SLOTS * m + s] = w[pair_index(i, j)]
    packed[ZTILES - 1, CTX_ROW:CTX_ROW + CTX] = w[FIELDS * (FIELDS - 1) // 2:]
    return packed


def kernel(**inputs):
    import concourse.bacc as bacc
    from concourse.bass_utils import run_bass_kernel_spmd

    ctx_rows = np.zeros((DIM, BATCH), np.float32)
    ctx_rows[CTX_ROW:CTX_ROW + CTX] = np.asarray(inputs["dense_ctx"]).T
    selectors = np.zeros((P, GROUP, DIM), np.float32)
    for p in range(P):
        selectors[p, np.arange(GROUP), SLOTS * np.arange(GROUP) + p // DIM] = 1
    arrays = {
        "ctx_rows": ctx_rows,
        "ids": np.asarray(inputs["ids"]),
        **{f"table{f}": np.asarray(inputs[f"tbl_{f}"]) for f in range(FIELDS)},
        "w_pairs": packed_weights(np.asarray(inputs["L0_rec_W"])),
        "eye": np.eye(P, dtype=np.float32),
        "selectors": selectors,
        "w1": packed_layer1(np.asarray(inputs["W_top1"])),
        "b1": np.ascontiguousarray(np.asarray(inputs["b_top1"]).reshape(M1, P).T),
        "w2": np.asarray(inputs["W_top2"]),
        "b2": np.ascontiguousarray(np.asarray(inputs["b_top2"]).reshape(M2, P).T),
        "w3": np.ascontiguousarray(np.asarray(inputs["W_top3"]).reshape(M2, P).T),
    }
    nc = bacc.Bacc("TRN2", target_bir_lowering=False, num_devices=1)
    aps = {name: nc.dram_tensor(name, a.shape, mybir.dt.from_np(a.dtype), kind="ExternalInput").ap()
           for name, a in arrays.items()}
    out = nc.dram_tensor("y", (BATCH, 1), F32, kind="ExternalOutput").ap()
    tables = [aps.pop(f"table{f}") for f in range(FIELDS)]
    build(nc, tables=tables, out=out, **aps)
    results = run_bass_kernel_spmd(nc, [arrays], core_ids=[0])
    return results.results[0]["y"]
```

```python
from contextlib import ExitStack

import concourse.bass as bass
import numpy as np
from concourse import mybir

F32 = mybir.dt.float32
F32R = mybir.dt.float32r
I32 = mybir.dt.int32
ALU = mybir.AluOpType
ACT = mybir.ActivationFunctionType

P = 128
BATCH = 512
CHUNKS = BATCH // P
FIELDS = 40
DIM = 32
SLOTS = P // DIM
QUADS = FIELDS // SLOTS
CTX = 16
HID1, HID2 = 512, 256
M1, M2 = HID1 // P, HID2 // P

ORDER = list(range(FIELDS))

RING_BANKS = 3
RING_P = 4
RING_ROWS = 12
RING_SPLIT = 3
RING_STREAM = 6
SPLIT_AT = (-1, 0, 4, 8, 12)
EARLY_FROM = 16
LIN_EVERY = (1, 1)
RING_W = 3
WCHUNKS = 5


def plan():
    ops_of = []
    for n in range(FIELDS):
        q, r = divmod(n, SLOTS)
        full = [(Q, [(n, tuple(range(SLOTS)))]) for Q in range(q)]
        ops = [full[i:i + 2] for i in range(0, len(full), 2)]
        if r == SLOTS - 1:
            a = SLOTS * q
            ops.append([(q, [(a + 3, (0, 1, 2))]), (q, [(a + 1, (0,)), (a + 2, (1,)), (a, (2,))])])
        ops_of.append(ops)
    return ops_of


OPS_OF = plan()
OPS = [op for ops in OPS_OF for op in ops]
TILES = [tile for op in OPS for tile in op]
FIRST_TILE = [sum(len(op) for op in OPS[:o]) for o in range(len(OPS))]
BLOCKS = [(t, stream, slots) for t, (quad, blocks) in enumerate(TILES) for stream, slots in blocks]
WBLOCKS = len(BLOCKS) // WCHUNKS
WPART = WBLOCKS // SLOTS
assert WBLOCKS * WCHUNKS == len(BLOCKS) and WPART * SLOTS == WBLOCKS

GROUP = DIM // SLOTS
ZTILE = SLOTS * GROUP
ZTILES = -(-len(TILES) // ZTILE)
CTX_ROW = 2 * SLOTS
assert (len(TILES) - ZTILE * (ZTILES - 1)) == CTX_ROW and CTX_ROW + CTX <= DIM


def z_place(t):
    return t // ZTILE, t % SLOTS, t % ZTILE // SLOTS


def pair_index(i, j):
    return i * FIELDS - i * (i + 1) // 2 + j - i - 1


def build(nc, ctx_rows, ids, tables, w_pairs, eye, selectors, w1, b1, w2, b2, w3, out):
    with ExitStack() as ctx:
        def sb(name, shape, dt=F32):
            return ctx.enter_context(nc.sbuf_tensor(name, shape, dt))

        def ps(name, shape):
            return ctx.enter_context(nc.psum_tensor(name, shape, F32))

        def sem(name):
            return ctx.enter_context(nc.semaphore(name))

        idx = sb("idx", [P, CHUNKS, FIELDS], I32)
        rows = sb("rows", [P, CHUNKS, RING_ROWS, DIM])
        split = sb("split", [P, RING_SPLIT, CHUNKS, 4, DIM], F32R)
        emb = sb("emb", [P, QUADS, BATCH])
        stream = sb("stream", [P, RING_STREAM, BATCH], F32R)
        wdense = sb("wdense", [P, 2, WPART * P])
        whi = sb("whi", [P, 2, WPART * P])
        wstack = sb("wstack", [P, RING_W, WBLOCKS * P], F32R)
        prod = sb("prod", [P, RING_P, 2 * BATCH])
        zt = sb("zt", [P, ZTILES, BATCH])
        w1_sb = sb("w1_sb", [P, ZTILES, HID1])
        w2_sb = sb("w2_sb", [P, M1, HID2])
        w3_sb = sb("w3_sb", [P, M2])
        b1_sb = sb("b1_sb", [P, M1])
        b2_sb = sb("b2_sb", [P, M2])
        ctx_sb = sb("ctx_sb", [DIM, BATCH])
        eye_sb = sb("eye_sb", [P, P])
        eye_r = sb("eye_r", [P, P], F32R)
        sel = sb("sel", [P, GROUP, DIM])
        h1 = sb("h1", [P, M1, BATCH])
        h2 = sb("h2", [P, M2, BATCH])
        y_sb = sb("y_sb", [1, BATCH])

        ring_ps = [ps(f"ring_ps{i}", [P, 2 * BATCH]) for i in range(RING_BANKS)]
        z_ps = ps("z_ps", [P, BATCH])
        lin_ps = ps("lin_ps", [P, BATCH])

        ids_loaded = sem("ids_loaded")
        const_loaded = sem("const_loaded")
        mlp_loaded = sem("mlp_loaded")
        wload = [sem(f"wload{i}") for i in range(WCHUNKS)]
        wstacked = [sem(f"wstacked{i}") for i in range(WCHUNKS)]
        gathered = [sem(f"gathered{n}") for n in range(FIELDS)]
        eye_ready = sem("eye_ready")
        whi_done = sem("whi_done")
        wlo_done = sem("wlo_done")
        hi_done = sem("hi_done")
        lo_done = sem("lo_done")
        turned = sem("turned")
        landed = sem("landed")
        mapped = sem("mapped")
        weighted = sem("weighted")
        summed = sem("summed")
        z_ended = sem("z_ended")
        ctx_placed = sem("ctx_placed")
        z_saved = sem("z_saved")
        lin_done = sem("lin_done")
        lin_saved = sem("lin_saved")
        last_added = sem("last_added")
        h1_ready = sem("h1_ready")
        h2_done = sem("h2_done")
        h2_ready = sem("h2_ready")
        y_done = sem("y_done")
        y_saved = sem("y_saved")
        stored = sem("stored")

        turn_of, turns = {}, 0
        for n in range(FIELDS):
            turn_of["field", n] = turns
            turns += 1
            if n % SLOTS == SLOTS - 1:
                turn_of["quad", n // SLOTS] = turns
                turns += 1
        op_index, o = [], 0
        for ops in OPS_OF:
            op_index.append(list(range(o, o + len(ops))))
            o += len(ops)
        NOPS = o
        LAST = NOPS - 1

        def op_of_tile(t):
            return max(o for o in range(NOPS) if FIRST_TILE[o] <= t)

        def last_op_of_chunk(c):
            return op_of_tile(BLOCKS[WBLOCKS * (c + 1) - 1][0])

        PARTS = [(0, 1, 2), (3, 4)]
        TAIL = (5, 6)
        turn_before = [max(op_index[n - 1][0], op_index[n - 1][-1] - 1) if n and op_index[n - 1] else
                       op_index[n][0] if op_index[n] else 0 for n in range(FIELDS)]
        for n in range(1, FIELDS):
            turn_before[n] = max(turn_before[n], turn_before[n - 1])

        turn_steps = [(turn_before[n] - 0.5, n, "turn", n) for n in range(FIELDS)]
        land_steps = [(turn_before[n] - 0.5, n, "land", n) for n in range(FIELDS)]
        for q in range(QUADS):
            n = SLOTS * q + SLOTS - 1
            at = max(turn_before[n] - 0.5, op_index[n][-1] - 3.5)
            turn_steps.append((at, n + 0.5, "turn_quad", q))
            land_steps.append((at, n + 0.5, "land_quad", q))
        hi_steps, lo_steps = [], []
        for n in range(FIELDS):
            behind = turn_before[max(n - 1, 0)] - 0.5
            early = n >= EARLY_FROM
            hi_steps.append((max(turn_before[n] - 5.5, behind), n - 1.5 if early else n - 0.5, "split", n))
            lo_steps.append((max(turn_before[n] - 3.5, behind), n - 0.5, "split", n))
        op_steps = [(o, 0, "op", o) for o in range(NOPS)]
        weight_steps = [(turn_before[max(n, 0)] - 0.5, n - 0.25, "weights", c) for c, n in enumerate(SPLIT_AT)]
        lin_steps, lin_save_steps = [], []
        for part, ks in enumerate(PARTS):
            at = op_of_tile(ZTILE * (ks[-1] + 1) - 1) + 5
            for m in range(M1):
                for k in ks:
                    lin_steps.append((at + 0.2, 0, "layer1", (part, m, k)))
                    at += LIN_EVERY[part]
                lin_save_steps.append((at - LIN_EVERY[part] + 1.2, 0, "save1", (part, m)))
                at += 1
        sums_after = {o: [s for s in (o - 3, o - 2) if s >= 0] for o in range(1, NOPS, 2)}
        left_sums = [o for o in range(NOPS) if not any(o in x for x in sums_after.values())]
        z_steps = [(o + 0.3, 0, "save_z", t // ZTILE) for o, sums in sums_after.items() for s in sums
                   for t in range(FIRST_TILE[s], FIRST_TILE[s] + len(OPS[s])) if (t + 1) % ZTILE == 0]

        pe_steps = sorted(turn_steps + op_steps + lin_steps)
        uses = [(kind, what) for _, _, kind, what in pe_steps if kind != "layer1"]
        ring_of = {use: ring_ps[i % RING_BANKS] for i, use in enumerate(uses)}
        before_in_ring = {use: uses[i - RING_BANKS] for i, use in enumerate(uses) if i >= RING_BANKS}

        z_ends_inside = [k for k in range(ZTILES - 1) if ZTILE * (k + 1) not in FIRST_TILE]

        def last_op_of_quad(q):
            return op_index[SLOTS * q + SLOTS - 1][-1]

        assert uses[-3:] == [("op", LAST - 2), ("op", LAST - 1), ("op", LAST)]
        older, old, newest = (ring_of["op", o] for o in (LAST - 2, LAST - 1, LAST))
        tail_ps = [lin_ps[:], older[:, :BATCH], older[:, BATCH:], old[:, :BATCH]]
        h2_ps = [old[:, BATCH:], newest[:, BATCH:]]
        y_ps = newest[0:1, :BATCH]

        block = ctx.enter_context(nc.Block())

        @block.sync
        def _(sp):
            sp.dma_start(idx[:], ids.rearrange("(c p) f -> p c f", p=P)).then_inc(ids_loaded, 16)

            def load_weights(c):
                if c >= 2:
                    sp.wait_ge(wstacked[c - 2], 16 * SLOTS * SLOTS)
                sp.dma_start(wdense[:, c % 2, :], w_pairs[c]).then_inc(wload[c], 16)

            def stack_weights(c):
                sp.wait_ge(whi_done, c + 1)
                sp.wait_ge(wlo_done, c + 1)
                if c >= RING_W:
                    sp.wait_ge(mapped, last_op_of_chunk(c - RING_W) + 1)
                n = WPART * P
                for k, part in enumerate((whi, wdense, whi, wdense)):
                    for q in range(SLOTS):
                        sp.dma_start(wstack[DIM * k:DIM * (k + 1), c % RING_W, q * n:(q + 1) * n].bitcast(F32),
                                     part[DIM * q:DIM * (q + 1), c % 2, :]).then_inc(wstacked[c], 16)

            load_weights(0)
            sp.dma_start(eye_sb[:], eye).then_inc(const_loaded, 16)
            sp.dma_start(sel[:], selectors).then_inc(const_loaded, 16)
            sp.dma_start(ctx_sb[:], ctx_rows).then_inc(const_loaded, 16)
            load_weights(1)
            for c in range(WCHUNKS):
                if c == RING_W:
                    sp.dma_start(w1_sb[:], w1.rearrange("k p n -> p k n")).then_inc(mlp_loaded, 16)
                    sp.dma_start(w2_sb[:], w2.rearrange("(k p) n -> p k n", p=P)).then_inc(mlp_loaded, 16)
                    sp.dma_start(w3_sb[:], w3).then_inc(mlp_loaded, 16)
                    sp.dma_start(b1_sb[:], b1).then_inc(mlp_loaded, 16)
                    sp.dma_start(b2_sb[:], b2).then_inc(mlp_loaded, 16)
                stack_weights(c)
                if c + 2 < WCHUNKS:
                    load_weights(c + 2)
            sp.wait_ge(y_saved, 1)
            sp.dma_start(out.rearrange("b o -> o b"), y_sb[:]).then_inc(stored, 16)
            sp.wait_ge(stored, 16)

        @block.gpsimd
        def _(pool):
            pool.wait_ge(ids_loaded, 16)
            for n, f in enumerate(ORDER):
                if n >= RING_ROWS and n % SLOTS == 0:
                    pool.wait_ge(turned, turn_of["quad", (n - RING_ROWS) // SLOTS] + 1)
                for c in range(CHUNKS):
                    nc.gpsimd.indirect_dma_start(
                        rows[:, c, n % RING_ROWS, :], None, tables[f],
                        bass.IndirectOffsetOnAxis(ap=idx[:, c, f:f + 1], axis=0)).then_inc(gathered[n], 16)

        @block.scalar
        def _(act):
            def weights(c):
                act.wait_ge(wload[c], 16)
                nc.scalar.activation(whi[:, c % 2, :].bitcast(F32R), wdense[:, c % 2, :], ACT.Copy).then_inc(whi_done, 1)

            def split_field(n):
                if n >= RING_SPLIT:
                    act.wait_ge(turned, turn_of["field", n - RING_SPLIT] + 1)
                act.wait_ge(gathered[n], 16 * CHUNKS)
                twice = rows[:, :, n % RING_ROWS, :].unsqueeze(2).to_broadcast([P, CHUNKS, 2, DIM])
                nc.scalar.activation(split[:, n % RING_SPLIT, :, 0:2, :], twice, ACT.Copy).then_inc(hi_done, 1)

            def land(n):
                if n >= RING_STREAM:
                    act.wait_ge(mapped, last_op_of_quad((n - RING_STREAM) // SLOTS) + 1)
                act.wait_ge(turned, turn_of["field", n] + 1)
                nc.scalar.activation(stream[:, n % RING_STREAM, :], ring_of["turn", n][:, :BATCH], ACT.Copy).then_inc(landed, 1)

            def land_quad(q):
                act.wait_ge(turned, turn_of["quad", q] + 1)
                nc.scalar.activation(emb[:, q, :], ring_of["turn_quad", q][:, :BATCH], ACT.Copy).then_inc(landed, 1)

            def save_z(k):
                if k in z_ends_inside:
                    act.wait_ge(z_ended, z_ends_inside.index(k) + 1)
                elif k < ZTILES - 1:
                    act.wait_ge(summed, op_of_tile(ZTILE * (k + 1) - 1) + 1)
                else:
                    act.wait_ge(ctx_placed, 1)
                nc.scalar.activation(zt[:, k, :], z_ps[:], ACT.Copy).then_inc(z_saved, 1)

            def layer1(part, m):
                if part == 0:
                    if m == 0:
                        act.wait_ge(mlp_loaded, 80)
                    act.wait_ge(lin_done, m + 1)
                    nc.scalar.activation(h1[:, m, :], lin_ps[:], ACT.Identity,
                                         bias=b1_sb[:, m:m + 1]).then_inc(lin_saved, 1)

            for _, _, kind, what in sorted(weight_steps + hi_steps + land_steps + z_steps + lin_save_steps):
                if kind == "weights":
                    weights(what)
                elif kind == "split":
                    split_field(what)
                elif kind == "land":
                    land(what)
                elif kind == "land_quad":
                    land_quad(what)
                elif kind == "save_z":
                    save_z(what)
                elif kind == "save1":
                    layer1(*what)
            save_z(ZTILES - 1)
            for m in range(M1):
                act.wait_ge(last_added, m + 1)
                nc.scalar.activation(h1[:, m, :], h1[:, m, :], ACT.Relu).then_inc(h1_ready, 1)
            for m in range(M2):
                act.wait_ge(h2_done, m + 1)
                nc.scalar.activation(h2[:, m, :], h2_ps[m], ACT.Relu,
                                     bias=b2_sb[:, m:m + 1]).then_inc(h2_ready, 1)

        @block.vector
        def _(dve):
            dve.wait_ge(const_loaded, 48)
            nc.vector.tensor_copy(eye_r[:], eye_sb[:]).then_inc(eye_ready, 1)

            def weights(c):
                dve.wait_ge(whi_done, c + 1)
                nc.vector.tensor_tensor(wdense[:, c % 2, :].bitcast(F32R), wdense[:, c % 2, :], whi[:, c % 2, :],
                                        ALU.subtract).then_inc(wlo_done, 1)

            def split_field(n):
                dve.wait_ge(hi_done, n + 1)
                twice = rows[:, :, n % RING_ROWS, :].unsqueeze(2).to_broadcast([P, CHUNKS, 2, DIM])
                nc.vector.tensor_tensor(split[:, n % RING_SPLIT, :, 2:4, :], twice,
                                        split[:, n % RING_SPLIT, :, 0:2, :], ALU.subtract).then_inc(lo_done, 1)

            def weight_op(o):
                op = OPS[o]
                quads = [quad for quad, _ in op]
                dve.wait_ge(landed, turn_of["quad", max(quads)] + 1)
                dve.wait_ge(mapped, o + 1)
                if o >= RING_P:
                    dve.wait_ge(summed, o - RING_P + 1)
                n = len(op) * BATCH
                if quads[-1] > quads[0] or len(op) == 1:
                    slots = emb[:, quads[0]:quads[-1] + 1, :]
                else:
                    slots = emb[:, quads[0]:quads[0] + 1, :].to_broadcast([P, 2, BATCH])
                shaped = "p (t b) -> p t b"
                nc.vector.tensor_tensor(prod[:, o % RING_P, :n].rearrange(shaped, b=BATCH),
                                        ring_of["op", o][:, :n].rearrange(shaped, b=BATCH), slots,
                                        ALU.mult).then_inc(weighted, 1)

            def layer1(part, m):
                if part == 1:
                    dve.wait_ge(lin_done, M1 + m + 1)
                    nc.vector.tensor_tensor(h1[:, m, :], lin_ps[:], h1[:, m, :], ALU.add).then_inc(lin_saved, 1)

            for _, _, kind, what in sorted(weight_steps + lo_steps + op_steps + lin_save_steps):
                if kind == "weights":
                    weights(what)
                elif kind == "split":
                    split_field(what)
                elif kind == "op":
                    weight_op(what)
                elif kind == "save1":
                    layer1(*what)
            for m in range(M1):
                dve.wait_ge(lin_done, len(PARTS) * M1 + m + 1)
                if m == 0:
                    dve.wait_ge(lin_saved, len(PARTS) * M1)
                nc.vector.tensor_tensor(h1[:, m, :], tail_ps[m], h1[:, m, :], ALU.add).then_inc(last_added, 1)
            dve.wait_ge(y_done, 1)
            nc.vector.tensor_copy(y_sb[:], y_ps).then_inc(y_saved, 1)

        @block.tensor
        def _(pe):
            used = [0]

            def ring_free(use):
                if use in before_in_ring:
                    kind, what = before_in_ring[use]
                    if kind == "op":
                        pe.wait_ge(weighted, what + 1)
                    else:
                        pe.wait_ge(landed, turn_of["field" if kind == "turn" else "quad", what] + 1)

            def turn(n):
                if n == 0:
                    pe.wait_ge(eye_ready, 1)
                pe.wait_ge(lo_done, n + 1)
                ring_free(("turn", n))
                for c in range(CHUNKS):
                    parts = split[:, n % RING_SPLIT, c].rearrange("p k d -> p (k d)")
                    mm = nc.tensor.matmul(ring_of["turn", n][:, c * P:(c + 1) * P], parts, eye_r[:], start=True, stop=True)
                mm.then_inc(turned, 1)

            def turn_quad(q):
                first = SLOTS * q % RING_ROWS
                ring_free(("turn_quad", q))
                for c in range(CHUNKS):
                    quad = rows[:, c, first:first + SLOTS, :].rearrange("p r d -> p (r d)")
                    mm = nc.tensor.matmul(ring_of["turn_quad", q][:, c * P:(c + 1) * P], quad, eye_sb[:],
                                          start=True, stop=True)
                mm.then_inc(turned, 1)

            def map_op(o):
                ring_free(("op", o))
                for i, (quad, blocks) in enumerate(OPS[o]):
                    for b, (n, slots) in enumerate(blocks):
                        c, w = divmod(used[0], WBLOCKS)
                        if w == 0:
                            pe.wait_ge(wstacked[c], 16 * SLOTS * SLOTS)
                        pe.wait_ge(landed, turn_of["field", n] + 1)
                        mm = nc.tensor.matmul(ring_of["op", o][:, i * BATCH:(i + 1) * BATCH],
                                              wstack[:, c % RING_W, w * P:(w + 1) * P],
                                              stream[:, n % RING_STREAM, :],
                                              start=b == 0, stop=b == len(blocks) - 1)
                        used[0] += 1
                return mm

            def sum_op(o):
                pe.wait_ge(weighted, o + 1)
                for i in range(len(OPS[o])):
                    t = FIRST_TILE[o] + i
                    k, g, m = z_place(t)
                    if t % ZTILE == 0 and k:
                        pe.wait_ge(z_saved, k)
                    last = m == GROUP - 1 or (t >= len(TILES) - SLOTS and g > 0)
                    mm = nc.tensor.matmul(z_ps[DIM * g:DIM * (g + 1), :], sel[:, m, :],
                                          prod[:, o % RING_P, i * BATCH:(i + 1) * BATCH], start=m == 0, stop=last)
                    if i == len(OPS[o]) - 1:
                        mm.then_inc(summed, 1)
                    elif t % ZTILE == ZTILE - 1:
                        mm.then_inc(z_ended, 1)

            def layer1(bank, ks, m, start=True, stop=True):
                for k in ks:
                    mm = nc.tensor.matmul(bank, w1_sb[:, k, m * P:(m + 1) * P], zt[:, k, :],
                                          start=start and k == ks[0], stop=stop and k == ks[-1])
                return mm

            pe.wait_ge(const_loaded, 48)
            for _, _, kind, what in pe_steps:
                if kind == "turn":
                    turn(what)
                elif kind == "turn_quad":
                    turn_quad(what)
                elif kind == "op":
                    map_op(what).then_inc(mapped, 1)
                    for o in sums_after.get(what, ()):
                        sum_op(o)
                elif kind == "layer1":
                    part, m, k = what
                    ks = PARTS[part]
                    if k == ks[0]:
                        pe.wait_ge(z_saved, ks[-1] + 1)
                        pe.wait_ge(mlp_loaded, 80)
                        if part or m:
                            pe.wait_ge(lin_saved, part * M1 + m)
                    mm = layer1(lin_ps[:], (k,), m, start=k == ks[0], stop=k == ks[-1])
                    if k == ks[-1]:
                        mm.then_inc(lin_done, 1)

            pe.wait_ge(z_saved, TAIL[0] + 1)
            pe.wait_ge(lin_saved, len(PARTS) * M1)
            layer1(tail_ps[0], TAIL[:1], 0, stop=False)
            pe.wait_ge(weighted, LAST - 1)
            layer1(tail_ps[1], TAIL[:1], 1, stop=False)
            for o in left_sums[:-1]:
                sum_op(o)
            layer1(tail_ps[2], TAIL[:1], 2, stop=False)
            layer1(tail_ps[3], TAIL[:1], 3, stop=False)
            sum_op(LAST)
            nc.tensor.matmul(z_ps[0:DIM, :], eye_sb[0:DIM, 0:DIM], ctx_sb[:],
                             start=False, stop=True).then_inc(ctx_placed, 1)
            pe.wait_ge(z_saved, ZTILES)
            for m in range(M1):
                layer1(tail_ps[m], TAIL[1:], m, start=False).then_inc(lin_done, 1)
            for k in range(M1):
                pe.wait_ge(h1_ready, k + 1)
                for m in range(M2):
                    mm = nc.tensor.matmul(h2_ps[m],
                                          w2_sb[:, k, m * P:(m + 1) * P], h1[:, k, :],
                                          start=k == 0, stop=k == M1 - 1)
                    if k == M1 - 1:
                        mm.then_inc(h2_done, 1)
            for k in range(M2):
                pe.wait_ge(h2_ready, k + 1)
                mm = nc.tensor.matmul(y_ps, w3_sb[:, k:k + 1], h2[:, k, :], start=k == 0, stop=k == M2 - 1)
            mm.then_inc(y_done, 1)


def packed_weights(w):
    packed = np.zeros((len(BLOCKS), DIM, SLOTS, DIM), w.dtype)
    for b, (t, stream, slots) in enumerate(BLOCKS):
        quad = TILES[t][0]
        for s in slots:
            slot_field, stream_field = ORDER[SLOTS * quad + s], ORDER[stream]
            if slot_field < stream_field:
                packed[b, :, s] = w[pair_index(slot_field, stream_field)].T
            else:
                packed[b, :, s] = w[pair_index(stream_field, slot_field)]
    packed = packed.reshape(WCHUNKS, SLOTS, WPART, DIM, P).transpose(0, 1, 3, 2, 4)
    return np.ascontiguousarray(packed.reshape(WCHUNKS, P, WPART * P))


def packed_layer1(w):
    packed = np.zeros((ZTILES, P, w.shape[1]), w.dtype)
    for t, stream, slots in BLOCKS:
        k, g, m = z_place(t)
        for s in slots:
            i, j = sorted((ORDER[SLOTS * TILES[t][0] + s], ORDER[stream]))
            packed[k, DIM * g + SLOTS * m + s] = w[pair_index(i, j)]
    packed[ZTILES - 1, CTX_ROW:CTX_ROW + CTX] = w[FIELDS * (FIELDS - 1) // 2:]
    return packed


def kernel(**inputs):
    import concourse.bacc as bacc
    from concourse.bass_utils import run_bass_kernel_spmd

    ctx_rows = np.zeros((DIM, BATCH), np.float32)
    ctx_rows[CTX_ROW:CTX_ROW + CTX] = np.asarray(inputs["dense_ctx"]).T
    selectors = np.zeros((P, GROUP, DIM), np.float32)
    for p in range(P):
        selectors[p, np.arange(GROUP), SLOTS * np.arange(GROUP) + p // DIM] = 1
    arrays = {
        "ctx_rows": ctx_rows,
        "ids": np.asarray(inputs["ids"]),
        **{f"table{f}": np.asarray(inputs[f"tbl_{f}"]) for f in range(FIELDS)},
        "w_pairs": packed_weights(np.asarray(inputs["L0_rec_W"])),
        "eye": np.eye(P, dtype=np.float32),
        "selectors": selectors,
        "w1": packed_layer1(np.asarray(inputs["W_top1"])),
        "b1": np.ascontiguousarray(np.asarray(inputs["b_top1"]).reshape(M1, P).T),
        "w2": np.asarray(inputs["W_top2"]),
        "b2": np.ascontiguousarray(np.asarray(inputs["b_top2"]).reshape(M2, P).T),
        "w3": np.ascontiguousarray(np.asarray(inputs["W_top3"]).reshape(M2, P).T),
    }
    nc = bacc.Bacc("TRN2", target_bir_lowering=False, num_devices=1)
    aps = {name: nc.dram_tensor(name, a.shape, mybir.dt.from_np(a.dtype), kind="ExternalInput").ap()
           for name, a in arrays.items()}
    out = nc.dram_tensor("y", (BATCH, 1), F32, kind="ExternalOutput").ap()
    tables = [aps.pop(f"table{f}") for f in range(FIELDS)]
    build(nc, tables=tables, out=out, **aps)
    results = run_bass_kernel_spmd(nc, [arrays], core_ids=[0])
    return results.results[0]["y"]
```

```python
from contextlib import ExitStack

import concourse.bass as bass
import numpy as np
from concourse import mybir

F32 = mybir.dt.float32
F32R = mybir.dt.float32r
I32 = mybir.dt.int32
ALU = mybir.AluOpType
ACT = mybir.ActivationFunctionType

P = 128
BATCH = 512
CHUNKS = BATCH // P
FIELDS = 40
DIM = 32
SLOTS = P // DIM
QUADS = FIELDS // SLOTS
CTX = 16
HID1, HID2 = 512, 256
M1, M2 = HID1 // P, HID2 // P

VOCAB = [1250, 1250, 125000, 12500, 12500, 125000, 12500, 12500, 12500, 1000, 1250, 1000, 1000, 1250, 1000,
         12500, 125000, 12500, 12500, 1250, 12500, 125000, 1250, 1000, 12500, 125000, 1250, 1000, 1000, 1250,
         1250, 125000, 12500, 1000, 1000, 1000, 1250, 1250, 12500, 1250]
HOT_VOCAB = 1000
N_HOT = 6
HOT_TILES = 8
HOT_ROWS = HOT_VOCAB // HOT_TILES
HOT = [f for f in range(FIELDS) if VOCAB[f] == HOT_VOCAB][:N_HOT]
GATHERED = [f for f in range(FIELDS) if f not in HOT]
ORDER = [f for pair in zip(HOT, GATHERED) for f in pair] + GATHERED[len(HOT):]
IS_HOT = [f in HOT for f in ORDER]
RANK = [sum(IS_HOT[:n]) if IS_HOT[n] else n - sum(IS_HOT[:n]) for n in range(FIELDS)]
HOT_AT = [n for n in range(FIELDS) if IS_HOT[n]]
GATHERED_AT = [n for n in range(FIELDS) if not IS_HOT[n]]

RING_BANKS = 3
RING_P = 6
RING_ROWS = 8
HOT_BY_ACT = 2
RING_ONE_HOT = 2
RING_TABLE = 2
RING_SPLIT = 3
RING_STREAM = 7
RING_DENSE = 3
RING_W = 4
WCHUNKS = 11
POOL_OPS = list(range(70, 96, 6))
assert all(o % 2 == 0 for o in POOL_OPS)
RING_COPY = 2
MLP_LOAD_AT = 4


def plan():
    ops_of = []
    for n in range(FIELDS):
        q, r = divmod(n, SLOTS)
        full = [(Q, [(n, tuple(range(SLOTS)))]) for Q in range(q)]
        ops = [full[i:i + 2] for i in range(0, q - q % 2, 2)]
        if q % 2 and r % 2:
            ops.append([(q - 1, [(n - 1, tuple(range(SLOTS)))]), full[-1]])
        if r == SLOTS - 1:
            a = SLOTS * q
            ops.append([(q, [(a + 3, (0, 1, 2))]), (q, [(a + 1, (0,)), (a + 2, (1,)), (a, (2,))])])
        ops_of.append(ops)
    return ops_of


OPS_OF = plan()
OPS = [op for ops in OPS_OF for op in ops]
TILES = [tile for op in OPS for tile in op]
BLOCKS = [(t, stream, slots) for t, (quad, blocks) in enumerate(TILES) for stream, slots in blocks]
WBLOCKS = len(BLOCKS) // WCHUNKS
WPART = WBLOCKS // SLOTS
assert WBLOCKS * WCHUNKS == len(BLOCKS) and WPART * SLOTS == WBLOCKS

GROUP = DIM // SLOTS
ZTILE = SLOTS * GROUP
ZTILES = -(-len(TILES) // ZTILE)
CTX_ROW = 2 * SLOTS
assert (len(TILES) - ZTILE * (ZTILES - 1)) == CTX_ROW and CTX_ROW + CTX <= DIM


def z_place(t):
    return t // ZTILE, t % SLOTS, t % ZTILE // SLOTS


PARTS = [(0, 1), (2,), (3,), (4,)]
TAIL = (5, 6)
NOPS = len(OPS)
assert NOPS % 2 == 0
FIRST_OP = [sum(map(len, OPS_OF[:n])) for n in range(FIELDS + 1)]
TURNS = [turn for q in range(QUADS)
         for turn in [("field", SLOTS * q + r) for r in range(SLOTS)] + [("quad", q)]]


def last_op_of_chunk(c):
    return BLOCKS[WBLOCKS * (c + 1) - 1][0] // 2


def step_order():
    steps = {
        "pe": [[("turn" if kind == "field" else "turn_quad", what) for kind, what in TURNS],
               [("op", o) for o in range(NOPS)],
               [("sum", b) for b in range(NOPS // 2 - 1)],
               [("layer1", (part, m, k)) for part, ks in enumerate(PARTS) for m in range(M1) for k in ks]],
        "act": [[("land" if kind == "field" else "land_quad", what) for kind, what in TURNS],
                [("copy", o) for o in POOL_OPS],
                [("hi", n) for n in range(FIELDS)],
                [("whi", c) for c in range(WCHUNKS)],
                [("one_hots", n) for n in HOT_AT],
                [("save_z", k) for k in range(ZTILES - 1)],
                [("save1", (0, m)) for m in range(M1)]],
        "dve": [[("lo", n) for n in range(FIELDS)],
                [("wlo", c) for c in range(WCHUNKS)],
                [("weight", o) for o in range(NOPS) if o not in POOL_OPS],
                [("save1", (part, m)) for part in range(1, len(PARTS)) for m in range(M1)]],
        "pool": [[("weight", o) for o in POOL_OPS]],
    }
    cost = {"turn": 0.3, "turn_quad": 0.9, "op": 0.45, "sum": 0.88, "layer1": 0.88,
            "land": 0.5, "land_quad": 0.5, "copy": 0.92, "hi": 0.35, "save_z": 0.55, "save1": 0.6,
            "whi": 0.65, "one_hots": 1.2 * HOT_BY_ACT, "lo": 0.35, "weight": 1.16, "wlo": 0.75}
    SIGNAL, GATHER, STACK = 0.4, 4.16, 10.5
    end, uses = {}, []

    def stream_free(n):
        return [("op", FIRST_OP[SLOTS * ((n - RING_STREAM) // SLOTS) + SLOTS] - 1)] if n >= RING_STREAM else []

    def issued(c):
        return max(end["wlo", c] + SIGNAL, issued(c - 1) + 0.7 if c else 0) + STACK

    def needs(kind, what):
        if kind == "hi":
            k, kinds = RANK[what], HOT_AT if IS_HOT[what] else GATHERED_AT
            ring = RING_TABLE if IS_HOT[what] else RING_SPLIT
            return ([("turn", kinds[k - ring])] if k >= ring else [],
                    6 + 2 * k if IS_HOT[what] else GATHER * (k + 1) + 5)
        if kind == "lo":
            k = RANK[what]
            return [("hi", what)] + ([("turn", HOT_AT[k - RING_ONE_HOT])] if IS_HOT[what] and k >= RING_ONE_HOT else []), 0
        if kind == "one_hots":
            k = RANK[what]
            return [("turn", HOT_AT[k - RING_ONE_HOT])] if k >= RING_ONE_HOT else [], 6 + 1.5 * k
        if kind == "whi":
            return ([("op", last_op_of_chunk(what - RING_W))] if what >= RING_W else []), \
                issued(what - 2) + 4 if what >= 2 else 5 + 11 * what
        if kind == "wlo":
            return [("whi", what)], 0
        if kind in ("turn", "turn_quad", "op"):
            ring = []
            if len(uses) >= RING_BANKS:
                k, w = uses[-RING_BANKS]
                ring = [({"turn": "land", "turn_quad": "land_quad", "op": "copy" if w in POOL_OPS else "weight"}[k], w)]
            if kind == "turn":
                return ring + stream_free(what) + [("lo", what)] + ([("one_hots", what)] if IS_HOT[what] else []), 0
            if kind == "turn_quad":
                return ring + [("land", SLOTS * what + r) for r in range(SLOTS)], 0
            blocks = [b for b in BLOCKS if b[0] // 2 == what]
            c = [i for i, b in enumerate(BLOCKS) if b[0] // 2 == what][-1] // WBLOCKS
            return (ring + [("land", n) for _, n, _ in blocks] + [("wlo", c), ("turn_quad", max(quad for quad, _ in OPS[what]))],
                    issued(c) + 2 if ("wlo", c) in end else 0)
        if kind == "land":
            return stream_free(what) + [("turn", what)], 0
        if kind == "land_quad":
            return [("turn_quad", what)], 0
        if kind == "copy":
            i = POOL_OPS.index(what)
            return [("op", what)] + ([("weight", POOL_OPS[i - RING_COPY])] if i >= RING_COPY else []), 0
        if kind == "weight":
            return ([("copy" if what in POOL_OPS else "op", what), ("land_quad", max(quad for quad, _ in OPS[what]))]
                    + ([("sum", (what - RING_P) // 2)] if what >= RING_P else [])), \
                4 + GATHER * len(GATHERED) if what in POOL_OPS else 0
        if kind == "sum":
            starts, k = divmod(what, GROUP)
            return [("weight", 2 * what), ("weight", 2 * what + 1)] + ([("save_z", starts - 1)] if k == 0 and starts else []), 0
        if kind == "save_z":
            return [("sum", GROUP * (what + 1) - 1)], 0
        if kind == "layer1":
            part, m, k = what
            if k != PARTS[part][0]:
                return [], 0
            return ([("save_z", PARTS[part][-1])]
                    + ([("save1", divmod(part * M1 + m - 1, M1))] if part or m else [])), 0
        part, m = what
        return [("layer1", (part, m, PARTS[part][-1]))], 0

    def duration(kind, what):
        if kind in ("hi", "lo", "turn") and IS_HOT[what]:
            return {"hi": 0.55, "lo": 0.7 + 0.41 * (HOT_TILES - HOT_BY_ACT), "turn": 1.8}[kind]
        if kind == "weight" and what in POOL_OPS:
            return 2.35
        return cost[kind]

    free = {engine: 0.0 for engine in steps}
    order = {engine: [] for engine in steps}
    while any(queue for queues in steps.values() for queue in queues):
        choices = []
        for engine, queues in steps.items():
            for priority, queue in enumerate(queues):
                if queue:
                    first, *_ = queue
                    try:
                        before, at = needs(*first)
                        ready = max([at] + [end[step] + SIGNAL for step in before])
                    except KeyError:
                        continue
                    choices.append((max(free[engine], ready), priority, engine))
        at, priority, engine = min(choices)
        step = steps[engine][priority].pop(0)
        order[engine].append(step)
        if step[0] in ("turn", "turn_quad", "op"):
            uses.append(step)
        end[step] = free[engine] = at + duration(*step)
    rename = {"hi": "split", "lo": "split", "whi": "weights", "wlo": "weights", "weight": "op"}
    return [[(rename.get(kind, kind), what) for kind, what in order[engine]] for engine in ("pe", "act", "dve")]


def pair_index(i, j):
    return i * FIELDS - i * (i + 1) // 2 + j - i - 1


def build(nc, ctx_rows, ids, ids_t, tables, w_pairs, eye, selectors, quad_selectors, vocab_rows, w1, b1, w2, b2, w3, out):
    with ExitStack() as ctx:
        def sb(name, shape, dt=F32):
            return ctx.enter_context(nc.sbuf_tensor(name, shape, dt))

        def ps(name, shape):
            return ctx.enter_context(nc.psum_tensor(name, shape, F32))

        def sem(name):
            return ctx.enter_context(nc.semaphore(name))

        idx = sb("idx", [P, CHUNKS, FIELDS], I32)
        rows = sb("rows", [P, CHUNKS, RING_ROWS, DIM])
        split = sb("split", [P, RING_SPLIT, CHUNKS, 4, DIM], F32R)
        emb = sb("emb", [P, QUADS, BATCH])
        stream = sb("stream", [P, RING_STREAM, BATCH], F32R)
        wdense = sb("wdense", [P, RING_DENSE, WPART * P])
        whi = sb("whi", [P, RING_DENSE, WPART * P])
        wstack = sb("wstack", [P, RING_W, WBLOCKS * P], F32R)
        prod = sb("prod", [P, RING_P, 2 * BATCH])
        zt = sb("zt", [P, ZTILES, BATCH])
        w3_sb = sb("w3_sb", [P, M2])
        b1_sb = sb("b1_sb", [P, M1])
        b2_sb = sb("b2_sb", [P, M2])
        ctx_sb = sb("ctx_sb", [P, BATCH])
        eye_sb = sb("eye_sb", [P, P])
        eye_r = sb("eye_r", [P, P], F32R)
        sel = sb("sel", [P, GROUP, DIM])
        quad_sel = sb("quad_sel", [P, SLOTS, P], F32R)
        vocab = sb("vocab", [P, 2, HOT_TILES])
        with ExitStack() as early:
            def early_sb(name, shape, dt=F32):
                return early.enter_context(nc.sbuf_tensor(name, shape, dt))

            quad_sel_in = early_sb("quad_sel_in", [P, SLOTS, P])
            hot_ids = early_sb("hot_ids", [P, N_HOT, BATCH], I32)
            hot_table = early_sb("hot_table", [P, N_HOT, HOT_TILES, DIM])
            hot_split = early_sb("hot_split", [P, RING_TABLE, HOT_TILES, 4, DIM], F32R)
            one_hot = early_sb("one_hot", [P, RING_ONE_HOT, HOT_TILES, BATCH], F32R)
            distance = early_sb("distance", [P, 2, BATCH])
        w1_sb = sb("w1_sb", [P, ZTILES, HID1])
        w2_sb = sb("w2_sb", [P, M1, HID2])
        h1 = sb("h1", [P, M1, BATCH])
        h2 = sb("h2", [P, M2, BATCH])
        y_sb = sb("y_sb", [1, BATCH])
        copied = sb("copied", [P, RING_COPY, 2 * BATCH])

        ring_ps = [ps(f"ring_ps{i}", [P, 2 * BATCH]) for i in range(RING_BANKS)]
        z_ps = ps("z_ps", [P, BATCH])
        lin_ps = ps("lin_ps", [P, BATCH])

        ids_loaded = sem("ids_loaded")
        vocab_loaded = sem("vocab_loaded")
        const_loaded = sem("const_loaded")
        sel_loaded = sem("sel_loaded")
        ctx_loaded = sem("ctx_loaded")
        mlp_loaded = sem("mlp_loaded")
        wload = [sem(f"wload{i}") for i in range(WCHUNKS)]
        wstacked = [sem(f"wstacked{i}") for i in range(WCHUNKS)]
        gathered = [sem(f"gathered{g}") for g in range(len(GATHERED))]
        hot_loaded = [sem(f"hot_loaded{h}") for h in range(len(HOT))]
        eye_ready = sem("eye_ready")
        hot_ready = sem("hot_ready")
        hot_ready_act = sem("hot_ready_act")
        distance_ready = sem("distance_ready")
        whi_done = sem("whi_done")
        wlo_done = sem("wlo_done")
        hi_done = sem("hi_done")
        lo_done = sem("lo_done")
        hot_lo_done = sem("hot_lo_done")
        turned = sem("turned")
        landed = sem("landed")
        mapped = sem("mapped")
        weighted = sem("weighted")
        copied_ready = sem("copied_ready")
        weighted_pool = sem("weighted_pool")
        summed = sem("summed")
        z_saved = sem("z_saved")
        last_z_saved = sem("last_z_saved")
        lin_done = sem("lin_done")
        lin_saved = sem("lin_saved")
        last_added = sem("last_added")
        h1_ready = sem("h1_ready")
        h2_done = sem("h2_done")
        h2_ready = sem("h2_ready")
        y_done = sem("y_done")
        y_saved = sem("y_saved")
        stored = sem("stored")

        turn_of = {turn: i for i, turn in enumerate(TURNS)}

        pe_steps, act_steps, dve_steps = step_order()

        uses = [step for step in pe_steps if step[0] in ("turn", "turn_quad", "op")]
        ring_of = {use: ring_ps[i % RING_BANKS] for i, use in enumerate(uses)}
        before_in_ring = {use: uses[i - RING_BANKS] for i, use in enumerate(uses) if i >= RING_BANKS}

        LAST = NOPS - 1

        def last_op_of_quad(q):
            return FIRST_OP[SLOTS * q + SLOTS] - 1

        assert uses[-3:] == [("op", LAST - 2), ("op", LAST - 1), ("op", LAST)]
        older, old, newest = (ring_of["op", o] for o in (LAST - 2, LAST - 1, LAST))
        tail_ps = [lin_ps[:], older[:, :BATCH], older[:, BATCH:], old[:, :BATCH]]
        h2_ps = [old[:, BATCH:], newest[:, BATCH:]]
        y_ps = newest[0:1, :BATCH]

        def by_pool(o):
            return sum(p <= o for p in POOL_OPS)

        def by_vector(o):
            return o + 1 - by_pool(o)

        def multiply(eng, o, products):
            quads = [quad for quad, _ in OPS[o]]
            if quads[1] > quads[0]:
                slots = emb[:, quads[0]:quads[0] + 2, :]
            else:
                slots = emb[:, quads[0]:quads[0] + 1, :].to_broadcast([P, 2, BATCH])
            shaped = "p (t b) -> p t b"
            return eng.tensor_tensor(prod[:, o % RING_P].rearrange(shaped, b=BATCH), products.rearrange(shaped, b=BATCH),
                                     slots, ALU.mult)

        block = ctx.enter_context(nc.Block())

        def load_hot(eng, h):
            f = HOT[h]
            eng.dma_start(hot_ids[:, h, :], ids_t[f:f + 1, :].to_broadcast([P, BATCH])
                          ).then_inc(hot_loaded[h], 16)
            eng.dma_start(hot_table[:HOT_ROWS, h].rearrange("p t d -> p (t d)"),
                          tables[f].rearrange("(p t) d -> p (t d)", t=HOT_TILES)).then_inc(hot_loaded[h], 16)

        @block.sync
        def _(sp):
            sp.dma_start(idx[:], ids.rearrange("(c p) f -> p c f", p=P)).then_inc(ids_loaded, 16)

            def load_weights(c):
                if c >= RING_DENSE:
                    sp.wait_ge(wstacked[c - RING_DENSE], 16 * SLOTS * SLOTS)
                sp.dma_start(wdense[:, c % RING_DENSE, :], w_pairs[c]).then_inc(wload[c], 16)

            def stack_weights(c):
                sp.wait_ge(whi_done, c + 1)
                sp.wait_ge(wlo_done, c + 1)
                if c >= RING_W:
                    sp.wait_ge(mapped, last_op_of_chunk(c - RING_W) + 1)
                n = WPART * P
                for k, part in enumerate((whi, wdense, whi, wdense)):
                    for q in range(SLOTS):
                        sp.dma_start(wstack[DIM * k:DIM * (k + 1), c % RING_W, q * n:(q + 1) * n].bitcast(F32),
                                     part[DIM * q:DIM * (q + 1), c % RING_DENSE, :]).then_inc(wstacked[c], 16)

            sp.dma_start(vocab[:], vocab_rows).then_inc(vocab_loaded, 16)
            load_hot(sp, 0)
            sp.dma_start(eye_sb[:], eye).then_inc(const_loaded, 16)
            load_weights(0)
            load_hot(sp, 1)
            sp.dma_start(quad_sel_in[:], quad_selectors).then_inc(const_loaded, 16)
            for h in range(2, N_HOT):
                load_hot(sp, h)
            sp.dma_start(sel[:], selectors).then_inc(sel_loaded, 16)
            load_weights(1)
            sp.dma_start(ctx_sb[:], ctx_rows).then_inc(ctx_loaded, 16)
            for c in range(WCHUNKS):
                if c == MLP_LOAD_AT:
                    sp.wait_ge(turned, turn_of["field", HOT_AT[-1]] + 1)
                    sp.dma_start(w1_sb[:], w1.rearrange("k p n -> p k n")).then_inc(mlp_loaded, 16)
                    sp.dma_start(w2_sb[:], w2.rearrange("(k p) n -> p k n", p=P)).then_inc(mlp_loaded, 16)
                    sp.dma_start(w3_sb[:], w3).then_inc(mlp_loaded, 16)
                    sp.dma_start(b1_sb[:], b1).then_inc(mlp_loaded, 16)
                    sp.dma_start(b2_sb[:], b2).then_inc(mlp_loaded, 16)
                stack_weights(c)
                if c + 2 < WCHUNKS:
                    load_weights(c + 2)
            sp.wait_ge(y_saved, 1)
            sp.dma_start(out.rearrange("b o -> o b"), y_sb[:]).then_inc(stored, 16)
            sp.wait_ge(stored, 16)

        @block.gpsimd
        def _(pool):
            pool.wait_ge(ids_loaded, 16)
            for g, n in enumerate(GATHERED_AT):
                f = ORDER[n]
                for c in range(CHUNKS):
                    if c == 0 and g >= RING_ROWS:
                        pool.wait_ge(lo_done, g - RING_ROWS + 1)
                    nc.gpsimd.indirect_dma_start(
                        rows[:, c, g % RING_ROWS, :], None, tables[f],
                        bass.IndirectOffsetOnAxis(ap=idx[:, c, f:f + 1], axis=0)).then_inc(gathered[g], 16)
            for i, o in enumerate(POOL_OPS):
                pool.wait_ge(landed, turn_of["quad", max(quad for quad, _ in OPS[o])] + 1)
                pool.wait_ge(copied_ready, i + 1)
                pool.wait_ge(summed, (o - RING_P) // 2 + 1)
                multiply(nc.gpsimd, o, copied[:, i % RING_COPY, :]).then_inc(weighted_pool, 1)

        @block.scalar
        def _(act):
            def weights(c):
                act.wait_ge(wload[c], 16)
                if c >= RING_DENSE:
                    act.wait_ge(wstacked[c - RING_DENSE], 16 * SLOTS * SLOTS)
                nc.scalar.activation(whi[:, c % RING_DENSE, :].bitcast(F32R), wdense[:, c % RING_DENSE, :], ACT.Copy).then_inc(whi_done, 1)

            def split_field(n):
                k = RANK[n]
                if IS_HOT[n]:
                    if k >= RING_TABLE:
                        act.wait_ge(turned, turn_of["field", HOT_AT[k - RING_TABLE]] + 1)
                    act.wait_ge(hot_loaded[k], 32)
                    twice = hot_table[:HOT_ROWS, k].unsqueeze(2).to_broadcast([HOT_ROWS, HOT_TILES, 2, DIM])
                    nc.scalar.activation(hot_split[:HOT_ROWS, k % RING_TABLE, :, 0:2, :], twice,
                                         ACT.Copy).then_inc(hi_done, 1)
                    return
                if k >= RING_SPLIT:
                    act.wait_ge(turned, turn_of["field", GATHERED_AT[k - RING_SPLIT]] + 1)
                act.wait_ge(gathered[k], 16 * CHUNKS)
                twice = rows[:, :, k % RING_ROWS, :].unsqueeze(2).to_broadcast([P, CHUNKS, 2, DIM])
                nc.scalar.activation(split[:, k % RING_SPLIT, :, 0:2, :], twice, ACT.Copy).then_inc(hi_done, 1)

            def one_hots(n):
                k = RANK[n]
                if k == 0:
                    act.wait_ge(vocab_loaded, 16)
                act.wait_ge(hot_loaded[k], 32)
                if k >= RING_ONE_HOT:
                    act.wait_ge(turned, turn_of["field", HOT_AT[k - RING_ONE_HOT]] + 1)
                first = HOT_BY_ACT * k

                def cut_off(i):
                    act.wait_ge(distance_ready, first + i + 1)
                    nc.scalar.activation(one_hot[:HOT_ROWS, k % RING_ONE_HOT, HOT_TILES - HOT_BY_ACT + i, :],
                                         distance[:HOT_ROWS, (first + i) % 2, :], ACT.Relu, scale=-1.0,
                                         bias=1.0).then_inc(hot_ready_act, 1)

                for i in range(HOT_BY_ACT):
                    if first + i >= 2:
                        act.wait_ge(hot_ready_act, first + i - 1)
                    t = HOT_TILES - HOT_BY_ACT + i
                    nc.scalar.activation(distance[:HOT_ROWS, (first + i) % 2, :], hot_ids[:HOT_ROWS, k, :], ACT.Abs,
                                         bias=vocab[:HOT_ROWS, 1, t:t + 1]).then_inc(distance_ready, 1)
                    if i:
                        cut_off(i - 1)
                cut_off(HOT_BY_ACT - 1)

            def land(n):
                if n >= RING_STREAM:
                    act.wait_ge(mapped, last_op_of_quad((n - RING_STREAM) // SLOTS) + 1)
                act.wait_ge(turned, turn_of["field", n] + 1)
                nc.scalar.activation(stream[:, n % RING_STREAM, :], ring_of["turn", n][:, :BATCH], ACT.Copy).then_inc(landed, 1)

            def land_quad(q):
                act.wait_ge(turned, turn_of["quad", q] + 1)
                nc.scalar.activation(emb[:, q, :], ring_of["turn_quad", q][:, :BATCH], ACT.Copy).then_inc(landed, 1)

            def copy_op(o):
                i = POOL_OPS.index(o)
                if i >= RING_COPY:
                    act.wait_ge(weighted_pool, i - RING_COPY + 1)
                else:
                    act.wait_ge(turned, turn_of["field", HOT_AT[-1]] + 1)
                act.wait_ge(mapped, o + 1)
                nc.scalar.activation(copied[:, i % RING_COPY, :], ring_of["op", o][:], ACT.Copy).then_inc(copied_ready, 1)

            def save_z(k):
                act.wait_ge(summed, GROUP * (k + 1))
                nc.scalar.activation(zt[:, k, :], z_ps[:], ACT.Copy).then_inc(z_saved, 1)

            def layer1(part, m):
                if part == 0:
                    if m == 0:
                        act.wait_ge(mlp_loaded, 80)
                    act.wait_ge(lin_done, m + 1)
                    nc.scalar.activation(h1[:, m, :], lin_ps[:], ACT.Identity,
                                         bias=b1_sb[:, m:m + 1]).then_inc(lin_saved, 1)

            for kind, what in act_steps:
                if kind == "weights":
                    weights(what)
                elif kind == "split":
                    split_field(what)
                elif kind == "one_hots":
                    one_hots(what)
                elif kind == "land":
                    land(what)
                elif kind == "land_quad":
                    land_quad(what)
                elif kind == "copy":
                    copy_op(what)
                elif kind == "save_z":
                    save_z(what)
                elif kind == "save1":
                    layer1(*what)
            for m in range(M1):
                act.wait_ge(last_added, m + 1)
                nc.scalar.activation(h1[:, m, :], h1[:, m, :], ACT.Relu).then_inc(h1_ready, 1)
            for m in range(M2):
                act.wait_ge(h2_done, m + 1)
                nc.scalar.activation(h2[:, m, :], h2_ps[m], ACT.Relu,
                                     bias=b2_sb[:, m:m + 1]).then_inc(h2_ready, 1)

        @block.vector
        def _(dve):
            def round_constants():
                dve.wait_ge(const_loaded, 32)
                nc.vector.tensor_copy(eye_r[:], eye_sb[:]).then_inc(eye_ready, 1)
                nc.vector.tensor_copy(quad_sel[:], quad_sel_in[:]).then_inc(eye_ready, 1)

            def weights(c):
                dve.wait_ge(whi_done, c + 1)
                nc.vector.tensor_tensor(wdense[:, c % RING_DENSE, :].bitcast(F32R), wdense[:, c % RING_DENSE, :], whi[:, c % RING_DENSE, :],
                                        ALU.subtract).then_inc(wlo_done, 1)

            def split_field(n):
                k = RANK[n]
                if IS_HOT[n]:
                    dve.wait_ge(hi_done, n + 1)
                    twice = hot_table[:HOT_ROWS, k].unsqueeze(2).to_broadcast([HOT_ROWS, HOT_TILES, 2, DIM])
                    parts = hot_split[:HOT_ROWS, k % RING_TABLE]
                    nc.vector.tensor_tensor(parts[:, :, 2:4, :], twice, parts[:, :, 0:2, :],
                                            ALU.subtract).then_inc(hot_lo_done, 1)
                    if k == 0:
                        dve.wait_ge(vocab_loaded, 16)
                    if k >= RING_ONE_HOT:
                        dve.wait_ge(turned, turn_of["field", HOT_AT[k - RING_ONE_HOT]] + 1)
                    for t in range(HOT_TILES - HOT_BY_ACT):
                        nc.vector.tensor_scalar(one_hot[:HOT_ROWS, k % RING_ONE_HOT, t, :], hot_ids[:HOT_ROWS, k, :],
                                                vocab[:HOT_ROWS, 0, t:t + 1], None, ALU.is_equal).then_inc(hot_ready, 1)
                    return
                dve.wait_ge(hi_done, n + 1)
                twice = rows[:, :, k % RING_ROWS, :].unsqueeze(2).to_broadcast([P, CHUNKS, 2, DIM])
                nc.vector.tensor_tensor(split[:, k % RING_SPLIT, :, 2:4, :], twice,
                                        split[:, k % RING_SPLIT, :, 0:2, :], ALU.subtract).then_inc(lo_done, 1)

            def weight_op(o):
                dve.wait_ge(landed, turn_of["quad", max(quad for quad, _ in OPS[o])] + 1)
                dve.wait_ge(mapped, o + 1)
                if o >= RING_P:
                    dve.wait_ge(summed, (o - RING_P) // 2 + 1)
                multiply(nc.vector, o, ring_of["op", o][:]).then_inc(weighted, 1)

            def layer1(part, m):
                if part:
                    dve.wait_ge(lin_done, M1 * part + m + 1)
                    nc.vector.tensor_tensor(h1[:, m, :], lin_ps[:], h1[:, m, :], ALU.add).then_inc(lin_saved, 1)

            for kind, what in dve_steps:
                if kind == "weights":
                    weights(what)
                elif kind == "split":
                    split_field(what)
                    if what == 0:
                        round_constants()
                elif kind == "op":
                    weight_op(what)
                elif kind == "save1":
                    layer1(*what)
            dve.wait_ge(ctx_loaded, 16)
            dve.wait_ge(summed, NOPS // 2)
            nc.vector.tensor_tensor(zt[:, ZTILES - 1, :], z_ps[:], ctx_sb[:], ALU.add).then_inc(last_z_saved, 1)
            for m in range(M1):
                dve.wait_ge(lin_done, len(PARTS) * M1 + m + 1)
                if m == 0:
                    dve.wait_ge(lin_saved, len(PARTS) * M1)
                nc.vector.tensor_tensor(h1[:, m, :], tail_ps[m], h1[:, m, :], ALU.add).then_inc(last_added, 1)
            dve.wait_ge(y_done, 1)
            nc.vector.tensor_copy(y_sb[:], y_ps).then_inc(y_saved, 1)

        @block.tensor
        def _(pe):
            used = [0]

            def ring_free(use):
                if use in before_in_ring:
                    kind, what = before_in_ring[use]
                    if kind == "op" and what in POOL_OPS:
                        pe.wait_ge(copied_ready, by_pool(what))
                    elif kind == "op":
                        pe.wait_ge(weighted, by_vector(what))
                    else:
                        pe.wait_ge(landed, turn_of["field" if kind == "turn" else "quad", what] + 1)

            def turn(n):
                if n == 1:
                    pe.wait_ge(eye_ready, 2)
                ring_free(("turn", n))
                k = RANK[n]
                if IS_HOT[n]:
                    pe.wait_ge(hot_lo_done, k + 1)
                    for t in range(HOT_TILES):
                        if t < HOT_TILES - HOT_BY_ACT:
                            pe.wait_ge(hot_ready, (HOT_TILES - HOT_BY_ACT) * k + t + 1)
                        else:
                            pe.wait_ge(hot_ready_act, HOT_BY_ACT * (k + 1) + t + 1 - HOT_TILES)
                        parts = hot_split[:HOT_ROWS, k % RING_TABLE, t].rearrange("p k d -> p (k d)")
                        mm = nc.tensor.matmul(ring_of["turn", n][:, :BATCH], parts, one_hot[:HOT_ROWS, k % RING_ONE_HOT, t, :],
                                              start=t == 0, stop=t == HOT_TILES - 1)
                    mm.then_inc(turned, 1)
                    return
                pe.wait_ge(lo_done, k + 1)
                for c in range(CHUNKS):
                    parts = split[:, k % RING_SPLIT, c].rearrange("p k d -> p (k d)")
                    mm = nc.tensor.matmul(ring_of["turn", n][:, c * P:(c + 1) * P], parts, eye_r[:], start=True, stop=True)
                mm.then_inc(turned, 1)

            def turn_quad(q):
                ring_free(("turn_quad", q))
                for r in range(SLOTS):
                    n = SLOTS * q + r
                    pe.wait_ge(landed, turn_of["field", n] + 1)
                    mm = nc.tensor.matmul(ring_of["turn_quad", q][:, :BATCH], quad_sel[:, r, :],
                                          stream[:, n % RING_STREAM, :], start=r == 0, stop=r == SLOTS - 1)
                mm.then_inc(turned, 1)

            def map_op(o):
                ring_free(("op", o))
                for i, (quad, blocks) in enumerate(OPS[o]):
                    for b, (n, slots) in enumerate(blocks):
                        c, w = divmod(used[0], WBLOCKS)
                        if w == 0:
                            pe.wait_ge(wstacked[c], 16 * SLOTS * SLOTS)
                        pe.wait_ge(landed, turn_of["field", n] + 1)
                        mm = nc.tensor.matmul(ring_of["op", o][:, i * BATCH:(i + 1) * BATCH],
                                              wstack[:, c % RING_W, w * P:(w + 1) * P],
                                              stream[:, n % RING_STREAM, :],
                                              start=b == 0, stop=b == len(blocks) - 1)
                        used[0] += 1
                return mm

            def sum_ops(b):
                if b == 0:
                    pe.wait_ge(sel_loaded, 16)
                pe.wait_ge(weighted, by_vector(2 * b + 1))
                if 2 * b in POOL_OPS:
                    pe.wait_ge(weighted_pool, by_pool(2 * b))
                for t in range(SLOTS * b, SLOTS * (b + 1)):
                    k, g, m = z_place(t)
                    if t % ZTILE == 0 and k:
                        pe.wait_ge(z_saved, k)
                    last = m == GROUP - 1 or t >= len(TILES) - SLOTS
                    mm = nc.tensor.matmul(z_ps[DIM * g:DIM * (g + 1), :], sel[:, m, :],
                                          prod[:, t // 2 % RING_P, t % 2 * BATCH:(t % 2 + 1) * BATCH],
                                          start=m == 0, stop=last)
                mm.then_inc(summed, 1)

            def layer1(bank, ks, m, start=True, stop=True):
                for k in ks:
                    mm = nc.tensor.matmul(bank, w1_sb[:, k, m * P:(m + 1) * P], zt[:, k, :],
                                          start=start and k == ks[0], stop=stop and k == ks[-1])
                return mm

            for kind, what in pe_steps:
                if kind == "turn":
                    turn(what)
                elif kind == "turn_quad":
                    turn_quad(what)
                elif kind == "op":
                    map_op(what).then_inc(mapped, 1)
                elif kind == "sum":
                    sum_ops(what)
                elif kind == "layer1":
                    part, m, k = what
                    ks = PARTS[part]
                    if k == ks[0]:
                        pe.wait_ge(z_saved, ks[-1] + 1)
                        pe.wait_ge(mlp_loaded, 80)
                        if part or m:
                            pe.wait_ge(lin_saved, part * M1 + m)
                    mm = layer1(lin_ps[:], (k,), m, start=k == ks[0], stop=k == ks[-1])
                    if k == ks[-1]:
                        mm.then_inc(lin_done, 1)

            pe.wait_ge(z_saved, TAIL[0] + 1)
            pe.wait_ge(lin_saved, len(PARTS) * M1)
            layer1(tail_ps[0], TAIL[:1], 0, stop=False)
            pe.wait_ge(weighted, by_vector(LAST - 2))
            layer1(tail_ps[1], TAIL[:1], 1, stop=False)
            pe.wait_ge(weighted, by_vector(LAST - 1))
            layer1(tail_ps[2], TAIL[:1], 2, stop=False)
            sum_ops(LAST // 2)
            layer1(tail_ps[3], TAIL[:1], 3, stop=False)
            pe.wait_ge(last_z_saved, 1)
            for m in range(M1):
                layer1(tail_ps[m], TAIL[1:], m, start=False).then_inc(lin_done, 1)
            for m in range(M2):
                for k in range(M1):
                    if m == 0:
                        pe.wait_ge(h1_ready, k + 1)
                    mm = nc.tensor.matmul(h2_ps[m], w2_sb[:, k, m * P:(m + 1) * P], h1[:, k, :],
                                          start=k == 0, stop=k == M1 - 1)
                mm.then_inc(h2_done, 1)
            for k in range(M2):
                pe.wait_ge(h2_ready, k + 1)
                mm = nc.tensor.matmul(y_ps, w3_sb[:, k:k + 1], h2[:, k, :], start=k == 0, stop=k == M2 - 1)
            mm.then_inc(y_done, 1)


def packed_weights(w):
    packed = np.zeros((len(BLOCKS), DIM, SLOTS, DIM), w.dtype)
    for b, (t, stream, slots) in enumerate(BLOCKS):
        quad = TILES[t][0]
        for s in slots:
            slot_field, stream_field = ORDER[SLOTS * quad + s], ORDER[stream]
            if slot_field < stream_field:
                packed[b, :, s] = w[pair_index(slot_field, stream_field)].T
            else:
                packed[b, :, s] = w[pair_index(stream_field, slot_field)]
    packed = packed.reshape(WCHUNKS, SLOTS, WPART, DIM, P).transpose(0, 1, 3, 2, 4)
    return np.ascontiguousarray(packed.reshape(WCHUNKS, P, WPART * P))


def packed_layer1(w):
    packed = np.zeros((ZTILES, P, w.shape[1]), w.dtype)
    for t, stream, slots in BLOCKS:
        k, g, m = z_place(t)
        for s in slots:
            i, j = sorted((ORDER[SLOTS * TILES[t][0] + s], ORDER[stream]))
            packed[k, DIM * g + SLOTS * m + s] = w[pair_index(i, j)]
    packed[ZTILES - 1, CTX_ROW:CTX_ROW + CTX] = w[FIELDS * (FIELDS - 1) // 2:]
    return packed


def kernel(**inputs):
    import concourse.bacc as bacc
    from concourse.bass_utils import run_bass_kernel_spmd

    ctx_rows = np.zeros((P, BATCH), np.float32)
    ctx_rows[CTX_ROW:CTX_ROW + CTX] = np.asarray(inputs["dense_ctx"]).T
    selectors = np.zeros((P, GROUP, DIM), np.float32)
    for p in range(P):
        selectors[p, np.arange(GROUP), SLOTS * np.arange(GROUP) + p // DIM] = 1
    quad_selectors = np.zeros((P, SLOTS, P), np.float32)
    for d in range(DIM):
        for slot in range(SLOTS):
            quad_selectors[[d, 2 * DIM + d], slot, DIM * slot + d] = 1
    vocab_rows = (HOT_TILES * np.arange(P)[:, None] + np.arange(HOT_TILES)).astype(np.float32)
    arrays = {
        "ctx_rows": ctx_rows,
        "ids": np.asarray(inputs["ids"]),
        **{f"table{f}": np.asarray(inputs[f"tbl_{f}"]) for f in range(FIELDS)},
        "w_pairs": packed_weights(np.asarray(inputs["L0_rec_W"])),
        "ids_t": np.ascontiguousarray(np.asarray(inputs["ids"]).T),
        "vocab_rows": np.stack([vocab_rows, -vocab_rows], axis=1),
        "quad_selectors": quad_selectors,
        "eye": np.eye(P, dtype=np.float32),
        "selectors": selectors,
        "w1": packed_layer1(np.asarray(inputs["W_top1"])),
        "b1": np.ascontiguousarray(np.asarray(inputs["b_top1"]).reshape(M1, P).T),
        "w2": np.asarray(inputs["W_top2"]),
        "b2": np.ascontiguousarray(np.asarray(inputs["b_top2"]).reshape(M2, P).T),
        "w3": np.ascontiguousarray(np.asarray(inputs["W_top3"]).reshape(M2, P).T),
    }
    nc = bacc.Bacc("TRN2", target_bir_lowering=False, num_devices=1)
    aps = {name: nc.dram_tensor(name, a.shape, mybir.dt.from_np(a.dtype), kind="ExternalInput").ap()
           for name, a in arrays.items()}
    out = nc.dram_tensor("y", (BATCH, 1), F32, kind="ExternalOutput").ap()
    tables = [aps.pop(f"table{f}") for f in range(FIELDS)]
    build(nc, tables=tables, out=out, **aps)
    results = run_bass_kernel_spmd(nc, [arrays], core_ids=[0])
    return results.results[0]["y"]
```
